# Optimizing a Trainium2 kernel written in Bass

```python
import numpy as np
import jax
import jax.numpy as jnp

def _softmax(x, axis=-1):
    return jax.nn.softmax(x, axis=axis)

def _gelu(x):
    return jax.nn.gelu(x, approximate=True)

def _silu(x):
    return jax.nn.silu(x)

def _sigmoid(x):
    return jax.nn.sigmoid(x)

def _layernorm(x, axis=-1, eps=1e-05):
    m = jnp.mean(x, axis=axis, keepdims=True)
    v = jnp.var(x, axis=axis, keepdims=True)
    return (x - m) / jnp.sqrt(v + eps)

def _scatter_add(tgt, idx, src, axis=0):
    return tgt.at[idx].add(src)

def _segment_sum(src, seg, n):
    return jax.ops.segment_sum(src, seg, n)
kernel_name = 'mk_cond_seq_d2_seqx_r8_71e28d'

def setup_inputs(seed: int=0):
    np.random.seed(seed)
    _w = jnp.asarray

    def _rec_inputs():
        import jax
        import jax.numpy as jnp
        _rk = jax.random.key(seed)
        x = 7.22e-05 + 1 * jax.random.normal(jax.random.fold_in(_rk, 1), (4, 256, 256), jnp.float32)
        _lenS = 256 - jax.random.randint(jax.random.fold_in(_rk, 7), (4,), 0, max(1, 256 // 4) + 1, jnp.int32)
        _lenS2 = 256 - jax.random.randint(jax.random.fold_in(_rk, 8), (4,), 0, max(1, 256 // 4) + 1, jnp.int32)
        cond_2048 = 0.0061147 + 1.02565 * jax.random.normal(jax.random.fold_in(_rk, 11), (4, 256), jnp.float32)
        _validS = jnp.arange(256)[None, :] < _lenS[:, None]
        _validS2 = jnp.arange(256)[None, :] < _lenS2[:, None]
        _causal = jnp.tril(jnp.ones((256, 256), dtype=bool))
        mask_1x1xSxS_ff0 = jnp.where(jnp.ones((1, 1, 256, 256), dtype=bool), 0.0, -1000000000.0).astype(jnp.float32)
        return (x, cond_2048, mask_1x1xSxS_ff0)
    x, cond_2048, mask_1x1xSxS_ff0 = _rec_inputs()

    def _L0_cond_setup():
        import jax, jax.numpy as jnp
        import numpy as np
        D_MODEL = 256
        N_HEADS = 16
        N_KV_HEADS = 4
        HEAD_DIM = D_MODEL // N_HEADS
        N_GROUPS = N_HEADS // N_KV_HEADS
        BLOCK_SIZE = 128
        WINDOW = 32
        GLOBAL_EVERY = 64
        LATENT = 64
        ROPE_THETA = 10000.0
        LN_EPS = 1e-05

        def _rope_tables(T, dtype):
            freqs = 1.0 / ROPE_THETA ** (jnp.arange(0, HEAD_DIM, 2, dtype=jnp.float32) / HEAD_DIM)
            emb = jnp.arange(T, dtype=jnp.float32)[:, None] * freqs[None, :]
            cos = jnp.concatenate([jnp.cos(emb), jnp.cos(emb)], axis=-1).astype(dtype)
            sin = jnp.concatenate([jnp.sin(emb), jnp.sin(emb)], axis=-1).astype(dtype)
            return (cos, sin)

        def _rotate_half(x):
            h = x.shape[-1] // 2
            return jnp.concatenate([-x[..., h:], x[..., :h]], axis=-1)

        def _sparse_mask(T):
            idx = jnp.arange(T)
            blk = idx // BLOCK_SIZE
            future_block = blk[None, :] > blk[:, None]
            outside_window = jnp.abs(idx[None, :] - idx[:, None]) > WINDOW
            global_visible = jnp.broadcast_to((idx % GLOBAL_EVERY == 0)[None, :], (T, T))
            return outside_window & ~global_visible | future_block
        key = jax.random.key(seed)
        ks = jax.random.split(key, 9)
        B, T = (2, 256)
        s = 0.02
        return {'x': jax.random.normal(ks[0], (B, T, D_MODEL), jnp.float32), 't_emb': jax.random.normal(ks[1], (B, D_MODEL), jnp.float32), 'W_ada': jax.random.normal(ks[2], (2 * D_MODEL, D_MODEL), jnp.float32) * s, 'b_ada': jnp.zeros((2 * D_MODEL,), jnp.float32), 'Wq': jax.random.normal(ks[3], (N_HEADS * HEAD_DIM, D_MODEL), jnp.float32) * s, 'Wkd': jax.random.normal(ks[4], (LATENT, D_MODEL), jnp.float32) * s, 'Wku': jax.random.normal(ks[5], (N_KV_HEADS * HEAD_DIM, LATENT), jnp.float32) * s, 'Wvu': jax.random.normal(ks[6], (N_KV_HEADS * HEAD_DIM, LATENT), jnp.float32) * s, 'Wo': jax.random.normal(ks[7], (D_MODEL, N_HEADS * HEAD_DIM), jnp.float32) * s}
    _L0_cond_all = _L0_cond_setup()
    _L0_cond_in = {k: v for k, v in _L0_cond_all.items() if k in ('W_ada', 'b_ada', 'Wq', 'Wkd', 'Wku', 'Wvu', 'Wo')}
    del _L0_cond_all

    def _L1_cond_setup():
        import jax, jax.numpy as jnp
        import numpy as np
        B, L, C, H = (2, 256, 256, 16)
        COND = 256
        HID = 4 * C
        LN_EPS = 1e-06

        def _ln(x):
            m = jnp.mean(x, axis=-1, keepdims=True)
            v = jnp.mean((x - m) ** 2, axis=-1, keepdims=True)
            return (x - m) / jnp.sqrt(v + LN_EPS)

        def _gelu_tanh(u):
            c = np.sqrt(2.0 / np.pi).astype(np.float32)
            return 0.5 * u * (1.0 + jnp.tanh(c * (u + 0.044715 * u ** 3)))
        key = jax.random.key(seed)
        ks = jax.random.split(key, 8)
        s = 0.02
        return {'x': jax.random.normal(ks[0], (B, L, C), jnp.float32), 'cond_BD': jax.random.normal(ks[1], (B, COND), jnp.float32), 'attn_bias': jnp.zeros((1, 1, L, L), jnp.float32), 'Wqkv': jax.random.normal(ks[2], (3 * C, C), jnp.float32) * s, 'q_bias': jnp.zeros((C,), jnp.float32), 'v_bias': jnp.zeros((C,), jnp.float32), 'scale_mul_log': jnp.full((1, H, 1, 1), np.log(4.0), jnp.float32), 'Wproj': jax.random.normal(ks[3], (C, C), jnp.float32) * s, 'bproj': jnp.zeros((C,), jnp.float32), 'Wada': jax.random.normal(ks[4], (6 * C, COND), jnp.float32) * s, 'bada': jnp.zeros((6 * C,), jnp.float32), 'Wfc1': jax.random.normal(ks[5], (HID, C), jnp.float32) * s, 'bfc1': jnp.zeros((HID,), jnp.float32), 'Wfc2': jax.random.normal(ks[6], (C, HID), jnp.float32) * s, 'bfc2': jnp.zeros((C,), jnp.float32)}
    _L1_cond_all = _L1_cond_setup()
    _L1_cond_in = {k: v for k, v in _L1_cond_all.items() if k in ('Wqkv', 'q_bias', 'v_bias', 'scale_mul_log', 'Wproj', 'bproj', 'Wada', 'bada', 'Wfc1', 'bfc1', 'Wfc2', 'bfc2')}
    del _L1_cond_all
    return {'x': x, 'cond_2048': cond_2048, 'mask_1x1xSxS_ff0': mask_1x1xSxS_ff0, 'L0_cond_W_ada': _L0_cond_in['W_ada'], 'L0_cond_b_ada': _L0_cond_in['b_ada'], 'L0_cond_Wq': _L0_cond_in['Wq'], 'L0_cond_Wkd': _L0_cond_in['Wkd'], 'L0_cond_Wku': _L0_cond_in['Wku'], 'L0_cond_Wvu': _L0_cond_in['Wvu'], 'L0_cond_Wo': _L0_cond_in['Wo'], 'L1_cond_Wqkv': _L1_cond_in['Wqkv'], 'L1_cond_q_bias': _L1_cond_in['q_bias'], 'L1_cond_v_bias': _L1_cond_in['v_bias'], 'L1_cond_scale_mul_log': _L1_cond_in['scale_mul_log'], 'L1_cond_Wproj': _L1_cond_in['Wproj'], 'L1_cond_bproj': _L1_cond_in['bproj'], 'L1_cond_Wada': _L1_cond_in['Wada'], 'L1_cond_bada': _L1_cond_in['bada'], 'L1_cond_Wfc1': _L1_cond_in['Wfc1'], 'L1_cond_bfc1': _L1_cond_in['bfc1'], 'L1_cond_Wfc2': _L1_cond_in['Wfc2'], 'L1_cond_bfc2': _L1_cond_in['bfc2']}

def reference(x, cond_2048, mask_1x1xSxS_ff0, L0_cond_W_ada, L0_cond_b_ada, L0_cond_Wq, L0_cond_Wkd, L0_cond_Wku, L0_cond_Wvu, L0_cond_Wo, L1_cond_Wqkv, L1_cond_q_bias, L1_cond_v_bias, L1_cond_scale_mul_log, L1_cond_Wproj, L1_cond_bproj, L1_cond_Wada, L1_cond_bada, L1_cond_Wfc1, L1_cond_bfc1, L1_cond_Wfc2, L1_cond_bfc2):
    import jax
    import jax.numpy as jnp

    def _L0_cond_ref(x, t_emb, W_ada, b_ada, Wq, Wkd, Wku, Wvu, Wo):
        import jax, jax.numpy as jnp
        import numpy as np
        D_MODEL = 256
        N_HEADS = 16
        N_KV_HEADS = 4
        HEAD_DIM = D_MODEL // N_HEADS
        N_GROUPS = N_HEADS // N_KV_HEADS
        BLOCK_SIZE = 128
        WINDOW = 32
        GLOBAL_EVERY = 64
        LATENT = 64
        ROPE_THETA = 10000.0
        LN_EPS = 1e-05

        def _rope_tables(T, dtype):
            freqs = 1.0 / ROPE_THETA ** (jnp.arange(0, HEAD_DIM, 2, dtype=jnp.float32) / HEAD_DIM)
            emb = jnp.arange(T, dtype=jnp.float32)[:, None] * freqs[None, :]
            cos = jnp.concatenate([jnp.cos(emb), jnp.cos(emb)], axis=-1).astype(dtype)
            sin = jnp.concatenate([jnp.sin(emb), jnp.sin(emb)], axis=-1).astype(dtype)
            return (cos, sin)

        def _rotate_half(x):
            h = x.shape[-1] // 2
            return jnp.concatenate([-x[..., h:], x[..., :h]], axis=-1)

        def _sparse_mask(T):
            idx = jnp.arange(T)
            blk = idx // BLOCK_SIZE
            future_block = blk[None, :] > blk[:, None]
            outside_window = jnp.abs(idx[None, :] - idx[:, None]) > WINDOW
            global_visible = jnp.broadcast_to((idx % GLOBAL_EVERY == 0)[None, :], (T, T))
            return outside_window & ~global_visible | future_block
        B, T, C = x.shape
        proj = t_emb @ W_ada.T + b_ada
        scale, shift = (proj[:, :C], proj[:, C:])
        mu = jnp.mean(x, axis=-1, keepdims=True)
        var = jnp.mean(jnp.square(x - mu), axis=-1, keepdims=True)
        h = (x - mu) * jax.lax.rsqrt(var + LN_EPS)
        h = h * (1.0 + scale[:, None, :]) + shift[:, None, :]
        q = (h @ Wq.T).reshape(B, T, N_HEADS, HEAD_DIM).transpose(0, 2, 1, 3)
        c_kv = h @ Wkd.T
        k = (c_kv @ Wku.T).reshape(B, T, N_KV_HEADS, HEAD_DIM).transpose(0, 2, 1, 3)
        v = (c_kv @ Wvu.T).reshape(B, T, N_KV_HEADS, HEAD_DIM).transpose(0, 2, 1, 3)
        cos, sin = _rope_tables(T, x.dtype)
        cos, sin = (cos[None, None], sin[None, None])
        q = q * cos + _rotate_half(q) * sin
        k = k * cos + _rotate_half(k) * sin
        k_exp = jnp.repeat(k, N_GROUPS, axis=1)
        v_exp = jnp.repeat(v, N_GROUPS, axis=1)
        mask = _sparse_mask(T)
        scores = jnp.einsum('bhtd,bhsd->bhts', q, k_exp) / jnp.sqrt(jnp.asarray(HEAD_DIM, x.dtype))
        scores = jnp.where(mask[None, None], jnp.asarray(-jnp.inf, x.dtype), scores)
        attn = jax.nn.softmax(scores, axis=-1)
        y = jnp.einsum('bhts,bhsd->bhtd', attn, v_exp)
        out = y.transpose(0, 2, 1, 3).reshape(B, T, C) @ Wo.T
        return x + out

    def _L1_cond_ref(x, cond_BD, attn_bias, Wqkv, q_bias, v_bias, scale_mul_log, Wproj, bproj, Wada, bada, Wfc1, bfc1, Wfc2, bfc2):
        import jax, jax.numpy as jnp
        import numpy as np
        B, L, C, H = (2, 256, 256, 16)
        COND = 256
        HID = 4 * C
        LN_EPS = 1e-06

        def _ln(x):
            m = jnp.mean(x, axis=-1, keepdims=True)
            v = jnp.mean((x - m) ** 2, axis=-1, keepdims=True)
            return (x - m) / jnp.sqrt(v + LN_EPS)

        def _gelu_tanh(u):
            c = np.sqrt(2.0 / np.pi).astype(np.float32)
            return 0.5 * u * (1.0 + jnp.tanh(c * (u + 0.044715 * u ** 3)))
        Bs, Lx, Cx = x.shape
        D = Cx // H
        ada = (jax.nn.silu(cond_BD) @ Wada.T + bada).reshape(Bs, 1, 6, Cx)
        gamma1, gamma2, scale1, scale2, shift1, shift2 = [ada[:, :, i, :] for i in range(6)]

        def attn(xin):
            qkv_bias = jnp.concatenate([q_bias, jnp.zeros_like(q_bias), v_bias])
            qkv = (xin @ Wqkv.T + qkv_bias).reshape(Bs, Lx, 3, H, D)
            qkv = jnp.transpose(qkv, (2, 0, 3, 1, 4))
            q, k, v = (qkv[0], qkv[1], qkv[2])
            sm = jnp.exp(jnp.minimum(scale_mul_log, jnp.log(jnp.float32(100.0))))
            qn = q / jnp.maximum(jnp.linalg.norm(q, axis=-1, keepdims=True), 1e-12) * sm
            kn = k / jnp.maximum(jnp.linalg.norm(k, axis=-1, keepdims=True), 1e-12)
            scores = jnp.einsum('bhqd,bhkd->bhqk', qn, kn) + attn_bias
            p = jax.nn.softmax(scores, axis=-1)
            o = jnp.einsum('bhqk,bhkd->bhqd', p, v)
            o = jnp.transpose(o, (0, 2, 1, 3)).reshape(Bs, Lx, Cx)
            return o @ Wproj.T + bproj
        x = x + attn(_ln(x) * (scale1 + 1.0) + shift1) * gamma1
        h = _gelu_tanh((_ln(x) * (scale2 + 1.0) + shift2) @ Wfc1.T + bfc1)
        x = x + (h @ Wfc2.T + bfc2) * gamma2
        return x
    x = _L0_cond_ref(x, cond_2048, L0_cond_W_ada, L0_cond_b_ada, L0_cond_Wq, L0_cond_Wkd, L0_cond_Wku, L0_cond_Wvu, L0_cond_Wo)
    x = _L1_cond_ref(x, cond_2048, mask_1x1xSxS_ff0, L1_cond_Wqkv, L1_cond_q_bias, L1_cond_v_bias, L1_cond_scale_mul_log, L1_cond_Wproj, L1_cond_bproj, L1_cond_Wada, L1_cond_bada, L1_cond_Wfc1, L1_cond_bfc1, L1_cond_Wfc2, L1_cond_bfc2)
    return x

_drawn_inputs = setup_inputs


def setup_inputs(seed=0):
    import zlib

    import numpy as np

    out = dict(_drawn_inputs(seed))
    spreads = {'L0_cond_b_ada': (0.0, 0.8),
     'L1_cond_q_bias': (0.0, 2.0),
     'L1_cond_v_bias': (0.0, 2.0),
     'L1_cond_scale_mul_log': (1.3862943649291992, 0.6),
     'L1_cond_bproj': (0.0, 2.0),
     'L1_cond_bada': (0.0, 0.404),
     'L1_cond_bfc1': (0.0, 2.0),
     'L1_cond_bfc2': (0.0, 2.0)}
    factors = {'L0_cond_W_ada': 8.0,
     'L0_cond_Wq': 8.0,
     'L0_cond_Wkd': 8.0,
     'L0_cond_Wku': 8.0,
     'L0_cond_Wvu': 8.0,
     'L0_cond_Wo': 8.0,
     'L1_cond_Wqkv': 8.0,
     'L1_cond_Wproj': 6.036,
     'L1_cond_Wfc1': 8.0,
     'L1_cond_Wfc2': 8.0}
    for name, (base, spread) in spreads.items():
        noise = np.random.default_rng([zlib.crc32(name.encode()), seed]).standard_normal(out[name].shape)
        drawn = base * np.exp(spread * noise) if base else spread * noise
        out[name] = jnp.asarray(drawn.astype(out[name].dtype))
    for name, factor in factors.items():
        out[name] = (out[name] * factor).astype(out[name].dtype)
    return out
```

```python
import concourse.bass as bass
from concourse import mybir
from contextlib import ExitStack

B, T, C = 4, 256, 256
P = 128
NT, NC = T // P, C // P
H, D, HKV = 16, 16, 4
GROUP = 4
NG = H // GROUP
HID = 4 * C
NF = HID // P
SLOT = 64
STACK = 3 * D
KVW = HKV * D
QK0 = C + KVW
W0 = C + 2 * KVW
NEG = -1e30
LOWEST = -3e38
LN0_EPS, LN1_EPS = 1e-5, 1e-6
ADA0, ADA1 = 4, 8
NADA = ADA0 + ADA1

SB = 0
TB = 2
OB = 6
MB = 7

S_USES = (3, 4)
FILLS = (5, 8)


def build(nc, x, condT, w_adaT, w_ada1T, b_adaT, b_gamma, wqT, wkd, wkuvT, woT, wqkvT, q_bias, v_bias,
          scale_log, wprojT, bproj, wfc1T, bfc1T, wfc2T, bfc2, bias_q, bias_k, ident_d, rope_d, hide_q_d,
          hide_k_d, sel_d, out):
    f32, f32r, bf16 = mybir.dt.float32, mybir.dt.float32r, mybir.dt.bfloat16
    ALU, ACT, AX = mybir.AluOpType, mybir.ActivationFunctionType, mybir.AxisListType

    ctx = ExitStack()
    with ctx:
        def sb(name, shape, dt=f32):
            return ctx.enter_context(nc.sbuf_tensor(name, shape, dt))

        def sem(name):
            return ctx.enter_context(nc.semaphore(name))

        condT_sb = sb("condT_sb", [P, NC, B])
        w_ada_sb = sb("w_ada_sb", [P, NC, 2 * C])
        w_ada1_sb = sb("w_ada1_sb", [P, NC, 6 * C])
        b_ada_sb = sb("b_ada_sb", [P, NADA])
        b_gamma_sb = sb("b_gamma_sb", [P, 2 * C])
        w0_sb = sb("w0_sb", [P, NC, W0])
        wkd_sb = sb("wkd_sb", [64, C])
        wkuv_sb = sb("wkuv_sb", [64, 2 * KVW])
        wo_sb = sb("wo_sb", [P, NC, C])
        wqkv_sb = sb("wqkv_sb", [P, NC, 3 * C])
        wproj_sb = sb("wproj_sb", [P, NC, C])
        wfc1_sb = sb("wfc1_sb", [P, NC, HID])
        wfc2_sb = sb("wfc2_sb", [P, NF, C])
        bfc1_sb = sb("bfc1_sb", [P, NF])
        qv_bias_sb = sb("qv_bias_sb", [P, 2, C])
        out_bias_sb = sb("out_bias_sb", [P, 2, C])
        scale_sb = sb("scale_sb", [P, H])
        ident = sb("ident", [P, P])
        ident_b = sb("ident_b", [P, P], bf16)
        ident_r = sb("ident_r", [P, P], f32r)
        rope = sb("rope", [P, NT, 2, D])
        hide_f = sb("hide_f", [P, 2, 384])
        hide_q = sb("hide_q", [P, 384], bf16)
        hide_k = sb("hide_k", [P, 384], bf16)
        sel_f = sb("sel_f", [2 * GROUP, GROUP, P])
        sel = sb("sel", [2 * GROUP, GROUP, P], f32r)
        bias_f = sb("bias_f", [P, 2, NT, T])
        bias_hi = sb("bias_hi", [P, 2, NT, T], f32r)
        bias_lo = sb("bias_lo", [P, 2, NT, T], f32r)
        silu_e = sb("silu_e", [P, NC, B])
        silu_d = sb("silu_d", [P, NC, B])
        silu_r = sb("silu_r", [P, NC, B])
        siluT = sb("siluT", [P, NC, B])
        silu_b = sb("silu_b", [P, NC, B, P])
        adaT = sb("adaT", [P, NADA, B])
        gamma = sb("gamma", [P, B, 2, C])
        sm_l = sb("sm_l", [P, H])
        sm = sb("sm", [P, H])
        x_in = sb("x_in", [P, NT, C])
        x1 = sb("x1", [P, NT, C])
        x1b = sb("x1b", [P, NT, C])
        bg = sb("bg", [P, C])
        x2 = sb("x2", [P, B, NT, C])
        ada_now = sb("ada_now", [P, NADA])
        stats = sb("stats", [P, NT, 6])
        mv = sb("mv", [P, NT, 2])
        wait_here = sb("wait_here", [P, 1])
        var_eps = sb("var_eps", [P, NT])
        rstd = sb("rstd", [P, NT])
        minus_half = sb("minus_half", [P, 2 * H])
        xn = sb("xn", [P, NT, C])
        hT = sb("hT", [P, NC, T])
        qk = sb("qk", [P, NT, 2 * C])
        qk_a = sb("qk_a", [P, NT, 2 * C])
        qk_b = sb("qk_b", [P, NT, 2 * C])
        ss = sb("ss", [P, NT, 2 * H])
        ss_min = sb("ss_min", [P, NT, 2 * H])
        rs = sb("rs", [P, NT, 2 * H])
        stack1 = sb("stack1", [P, NT, 2 * H, SLOT])
        stack = [stack1[:, :, 0:H + HKV, :], stack1[:]]
        qkT1 = sb("qkT1", [P, H, T], f32r)
        qkT = [qkT1[:, 0:(H + HKV) // 2, :], qkT1[:]]
        vaug = [sb("vaug0", [P, NT, HKV, 2 * D]), sb("vaug1", [P, NT, H, 2 * D])]
        negmax = sb("negmax", [P, H, NT])
        m_parts = sb("m_parts", [P, NG, NT, GROUP, 2])
        mT = sb("mT", [2 * GROUP, 2, 3 * P], f32r)
        prob = sb("prob", [P, 2, GROUP, 2 * T])
        oT_raw = sb("oT_raw", [P, T])
        den = sb("den", [P, NT, GROUP])
        o = sb("o", [P, NT, C])
        oT = sb("oT", [P, NC, T])
        scaled = sb("scaled", [P, NT, C])
        gT = prob[:].rearrange("p a h q -> p (a h q)")[:, 0:NF * T].rearrange("p (f q) -> p f q", f=NF)
        x2b = sb("x2b", [P, NT, C])
        ps = ctx.enter_context(nc.psum_tensor("ps", [P, 8, 512], f32))

        cond_in, consts_in, late_in = sem("cond_in"), sem("consts_in"), sem("late_in")
        mlp_in = sem("mlp_in")
        silu_exp, silu_ready, sm_ready = sem("silu_exp"), sem("silu_ready"), sem("sm_ready")
        dve_setup, sm_min = sem("dve_setup"), sem("sm_min")
        setup_mm, setup_dve, pads_set = sem("setup_mm"), sem("setup_dve"), sem("pads_set")
        x_loaded = sem("x_loaded")

        def two(name):
            return [sem(name + "0"), sem(name + "1")]
        dve_seq, pool_seq = sem("dve_seq"), sem("pool_seq")
        xn_ready, xnT_done, hT_ready = two("xn_ready"), two("xnT_done"), two("hT_ready")
        proj_in_done, raw_ready, stack_ready = two("proj_in_done"), sem("raw_ready"), two("stack_ready")
        k1_ready, q1_ready = sem("k1_ready"), sem("q1_ready")
        squares_ready, ss_ready, rs_ready = sem("squares_ready"), sem("ss_ready"), sem("rs_ready")
        var_ready, rstd_ready = two("var_ready"), two("rstd_ready")
        var2_ready, rstd2_ready = sem("var2_ready"), sem("rstd2_ready")
        fill_done, fill_act, fill_dve = two("fill_done"), two("fill_act"), two("fill_dve")
        s_done, max_done, m_ready = two("s_done"), two("max_done"), two("m_ready")
        mT_done, mT_ready, st_done, exp_done = two("mT_done"), two("mT_ready"), two("st_done"), two("exp_done")
        av_done, oT_evac, otr_done, o_ready = two("av_done"), two("oT_evac"), two("otr_done"), two("o_ready")
        oc_done, oc_ready, proj_done, x_ready = two("oc_done"), two("oc_ready"), two("proj_done"), two("x_ready")
        x1b_ready, scaled_ready = sem("x1b_ready"), sem("scaled_ready")
        ln2_seq, xn2_ready, xn2T_done, h2T_ready = sem("ln2_seq"), sem("xn2_ready"), sem("xn2T_done"), sem("h2T_ready")
        fc1_done, gelu_done, fc2_done, y_ready = sem("fc1_done"), sem("gelu_done"), sem("fc2_done"), sem("y_ready")
        x2b_ready, y_stored = sem("x2b_ready"), sem("y_stored")

        DVE_SEQ = 43
        SETUP_MM = 10
        COND_IN, CONSTS_IN, LATE_IN, MLP_IN = 5 * 16, 11 * 16, 11 * 16, 4 * 16
        block = ctx.enter_context(nc.Block())

        x_v = x.rearrange("b (t p) c -> b p t c", p=P)
        out_v = out.rearrange("b (t p) c -> b p t c", p=P)

        def wide(w):
            return w.rearrange("(k p) n -> p k n", p=P)

        def rows(v):
            return v.partition_broadcast(P)

        @block.sync
        def _(sp):
            sp.dma_start(condT_sb[:], condT.rearrange("(k p) b -> p k b", p=P)).then_inc(cond_in, 16)
            sp.dma_start(x_in[:], x_v[0]).then_inc(x_loaded, 16)
            sp.dma_start(ident[:], ident_d).then_inc(consts_in, 16)
            sp.dma_start(w_ada_sb[:], wide(w_adaT)).then_inc(cond_in, 16)
            sp.dma_start(w_ada1_sb[:], wide(w_ada1T)).then_inc(cond_in, 16)
            sp.dma_start(b_ada_sb[:], b_adaT).then_inc(cond_in, 16)
            sp.dma_start(b_gamma_sb[:], rows(b_gamma)).then_inc(cond_in, 16)
            sp.dma_start(wkd_sb[:], wkd).then_inc(consts_in, 16)
            sp.dma_start(wkuv_sb[:], wkuvT).then_inc(consts_in, 16)
            sp.dma_start(w0_sb[:, :, 0:C], wide(wqT)).then_inc(consts_in, 16)
            sp.dma_start(rope[:], rope_d.rearrange("(t p) a d -> p t a d", p=P)).then_inc(consts_in, 16)
            sp.dma_start(hide_f[:, 0, :], hide_q_d).then_inc(consts_in, 16)
            sp.dma_start(hide_f[:, 1, :], hide_k_d).then_inc(consts_in, 16)
            sp.dma_start(sel_f[:], sel_d).then_inc(consts_in, 16)
            sp.dma_start(wo_sb[:], wide(woT)).then_inc(consts_in, 16)
            sp.dma_start(bias_f[:, 0], bias_q.rearrange("(t p) k -> p t k", p=P)).then_inc(consts_in, 16)
            sp.dma_start(bias_f[:, 1], bias_k.rearrange("(t p) k -> p t k", p=P)).then_inc(consts_in, 16)
            with sp.Fori(1, B) as i:
                sp.wait_ge(x_ready[0], i * NT)
                sp.dma_start(x_in[:], x_v[i]).then_inc(x_loaded, 16)
            with sp.Fori(0, B) as i:
                sp.wait_ge(y_ready, i * NT + NT)
                sp.dma_start(out_v[i], x2[:, i]).then_inc(y_stored, 16)
            sp.wait_ge(y_stored, B * 16)

        @block.gpsimd
        def _(pool):
            pool.memset(stack1[:, :, :, STACK:SLOT], 0.0).then_inc(pads_set, 1)
            for v in vaug:
                pool.memset(v[:, :, :, D:2 * D], 1.0).then_inc(pads_set, 1)
            pool.memset(minus_half[:], -0.5).then_inc(pads_set, 1)
            pool.wait_ge(pads_set, 4)

            def inverse_root(i, ready, done):
                pool.wait_ge(ready, i + 1)
                pool.tensor_tensor(rstd[:], var_eps[:], minus_half[:, 0:NT], ALU.pow).then_inc(done, 1)

            with pool.Fori(0, B) as i:
                inverse_root(i, var_ready[0], rstd_ready[0])
                inverse_root(i, var_ready[1], rstd_ready[1])
                pool.wait_ge(x_ready[0], i * NT + NT)
                pool.tensor_tensor(bg[:], out_bias_sb[:, 0], gamma[:, i, 0, :], ALU.mult).then_inc(pool_seq, 1)
                pool.wait_ge(pool_seq, i + 1)
                pool.tensor_tensor(x1b[:], x1[:], bg[:].unsqueeze(1).to_broadcast([P, NT, C]),
                                   ALU.add).then_inc(x1b_ready, 1)
                for t in range(NT):
                    pool.wait_ge(ss_ready, i * NT + t + 1)
                    pool.tensor_tensor(rs[:, t, :], ss_min[:, t, :], minus_half[:], ALU.pow).then_inc(rs_ready, 1)
            with pool.Fori(0, B) as i:
                inverse_root(i, var2_ready, rstd2_ready)
                pool.tensor_tensor(bg[:], out_bias_sb[:, 1], gamma[:, i, 1, :], ALU.mult).then_inc(pool_seq, 1)
                pool.wait_ge(pool_seq, B + i + 1)
                pool.tensor_tensor(x2b[:], x2[:, i], bg[:].unsqueeze(1).to_broadcast([P, NT, C]),
                                   ALU.add).then_inc(x2b_ready, 1)

        @block.scalar
        def _(act):
            act.dma_start(scale_sb[:], rows(scale_log)).then_inc(late_in, 16)
            act.dma_start(wqkv_sb[:, 0, :], wqkvT[0:P, :]).then_inc(late_in, 16)
            act.dma_start(wqkv_sb[:, 1, :], wqkvT[P:C, :]).then_inc(late_in, 16)
            act.dma_start(qv_bias_sb[:, 0], rows(q_bias)).then_inc(late_in, 16)
            act.dma_start(qv_bias_sb[:, 1], rows(v_bias)).then_inc(late_in, 16)
            act.dma_start(out_bias_sb[:, 0], rows(bproj)).then_inc(late_in, 16)
            act.dma_start(out_bias_sb[:, 1], rows(bfc2)).then_inc(late_in, 16)
            act.dma_start(wproj_sb[:], wide(wprojT)).then_inc(late_in, 16)
            act.dma_start(bfc1_sb[:], bfc1T).then_inc(late_in, 16)
            act.dma_start(wfc1_sb[:], wide(wfc1T)).then_inc(late_in, 16)
            act.dma_start(wfc2_sb[:], wide(wfc2T)).then_inc(late_in, 16)
            act.wait_ge(cond_in, COND_IN)
            nc.scalar.activation(silu_e[:], condT_sb[:], ACT.Exp, scale=-1.0).then_inc(silu_exp, 1)
            act.wait_ge(sm_min, 1)
            nc.scalar.activation(sm[:], sm_l[:], ACT.Exp).then_inc(sm_ready, 1)

            def attention(i, L):
                act.wait_ge(xnT_done[L], i + 1)
                for c in range(NC):
                    scale, shift = (c, 2 + c) if L == 0 else (ADA0 + c, ADA0 + 4 + c)
                    nc.scalar.activation(hT[:, c, :], ps[:, MB, c * T:(c + 1) * T], ACT.Identity,
                                         bias=ada_now[:, shift:shift + 1],
                                         scale=ada_now[:, scale:scale + 1]).then_inc(hT_ready[L], 1)
                for t in range(NT):
                    act.wait_ge(proj_in_done[L], i * NT + t + 1)
                    if L == 0:
                        nc.scalar.activation(vaug[0][:, t, :, 0:D],
                                             ps[:, SB + t, QK0:W0].rearrange("p (g d) -> p g d", d=D), ACT.Copy)
                        nc.scalar.activation(qk[:, t, 0:QK0], ps[:, SB + t, 0:QK0],
                                             ACT.Copy).then_inc(raw_ready, 1)
                    else:
                        nc.scalar.activation(qk[:, t, C:2 * C], ps[:, 2 * t, C:2 * C],
                                             ACT.Copy).then_inc(k1_ready, 1)
                if L == 1:
                    for t in range(NT):
                        act.wait_ge(k1_ready, i * NT + t + 1)
                        act.wait_ge(q1_ready, i * NT + t + 1)
                        nc.scalar.activation(qk_a[:, t, :], qk[:, t, :], ACT.Square).then_inc(squares_ready, 1)
                for n in range(0, FILLS[L], 2):
                    act.wait_ge(fill_done[L], i * FILLS[L] + n + 1)
                    nc.scalar.activation(qkT[L][:, 2 * FILL_ORDER[L][n]:2 * FILL_ORDER[L][n] + 2, :],
                                         ps[:, FILL_BANK[L][n], :], ACT.Copy).then_inc(fill_act[L], 1)
                cols = 3 * P if L == 0 else 2 * T
                for g in range(NG):
                    width = 3 * P if L == 0 else T
                    act.wait_ge(mT_done[L], i * NG + g + 1)
                    nc.scalar.activation(mT[:, g % 2, 0:width], ps[0:2 * GROUP, MB, 0:width],
                                         ACT.Copy).then_inc(mT_ready[L], 1)
                    for p in range(2):
                        n = 2 * g + p
                        if p == 0 and g >= 2:
                            act.wait_ge(av_done[L], i * NG + g - 1)
                        act.wait_ge(st_done[L], i * 2 * NG + n + 1)
                        nc.scalar.activation(prob[:, g % 2, 2 * p:2 * p + 2, 0:cols],
                                             ps[:, TB + 2 * p:TB + 2 * p + 2, 0:cols], ACT.Exp,
                                             scale=D ** -0.5 if L == 0 else 1.0).then_inc(exp_done[L], 1)
                act.wait_ge(oc_done[L], i + 1)
                nc.scalar.activation(oT[:], ps[:, MB, :], ACT.Copy).then_inc(oc_ready[L], 1)

            with act.Fori(0, B) as i:
                attention(i, 0)
                attention(i, 1)

            with act.Fori(0, B) as i:
                act.wait_ge(xn2T_done, i + 1)
                for c in range(NC):
                    nc.scalar.activation(hT[:, c, :], ps[:, MB, c * T:(c + 1) * T], ACT.Identity,
                                         bias=ada_now[:, ADA0 + 6 + c:ADA0 + 7 + c],
                                         scale=ada_now[:, ADA0 + 2 + c:ADA0 + 3 + c]).then_inc(h2T_ready, 1)
                for f in range(NF):
                    act.wait_ge(fc1_done, i * NF + f + 1)
                    nc.scalar.activation(gT[:, f, :], ps[:, 2 + f % 4, 0:T], ACT.Gelu_apprx_tanh,
                                         bias=bfc1_sb[:, f:f + 1]).then_inc(gelu_done, 1)

        @block.vector
        def _(dve):
            n = [0]

            def seq(i, ins):
                n[0] += 1
                ins.then_inc(dve_seq, 1)
                dve.wait_ge(dve_seq, i * DVE_SEQ + n[0])

            setup = [0]

            def done(ins):
                setup[0] += 1
                ins.then_inc(dve_setup, 1)
                dve.wait_ge(dve_setup, setup[0])

            dve.wait_ge(silu_exp, 1)
            done(nc.vector.tensor_scalar(silu_d[:], silu_e[:], 1.0, None, ALU.add))
            done(nc.vector.reciprocal(silu_r[:], silu_d[:]))
            done(nc.vector.tensor_tensor(siluT[:], condT_sb[:], silu_r[:], ALU.mult))
            nc.vector.tensor_copy(silu_b[:], siluT[:].unsqueeze(3).to_broadcast([P, NC, B, P])).then_inc(silu_ready, 1)
            dve.wait_ge(consts_in, CONSTS_IN)
            nc.vector.tensor_copy(ident_b[:], ident[:]).then_inc(setup_dve, 1)
            nc.vector.tensor_copy(ident_r[:], ident[:]).then_inc(setup_dve, 1)
            nc.vector.tensor_copy(hide_q[:], hide_f[:, 0, :]).then_inc(setup_dve, 1)
            nc.vector.tensor_copy(hide_k[:], hide_f[:, 1, :]).then_inc(setup_dve, 1)
            nc.vector.tensor_copy(sel[:], sel_f[:]).then_inc(setup_dve, 1)
            done(nc.vector.tensor_scalar(bias_f[:], bias_f[:], LOWEST, None, ALU.max))
            done(nc.vector.tensor_copy(bias_hi[:], bias_f[:]))
            nc.vector.tensor_tensor(bias_lo[:], bias_f[:], bias_hi[:].bitcast(f32), ALU.subtract).then_inc(setup_dve, 1)
            dve.wait_ge(late_in, LATE_IN)
            nc.vector.tensor_scalar(sm_l[:], scale_sb[:], 4.605170185988092, None, ALU.min).then_inc(sm_min, 1)
            dve.wait_ge(setup_mm, 1)
            done(nc.vector.tensor_tensor(adaT[:], ps[:, 0, 0:NADA * B].rearrange("p (a b) -> p a b", b=B),
                                         b_ada_sb[:].unsqueeze(2).to_broadcast([P, NADA, B]), ALU.add))
            for first, count in ((0, 2), (ADA0, 4)):
                done(nc.vector.tensor_scalar(adaT[:, first:first + count, :], adaT[:, first:first + count, :],
                                             1.0, None, ALU.add))
            dve.wait_ge(setup_mm, 2)
            nc.vector.tensor_copy(w0_sb[:, :, C:W0], ps[:, 1, 0:NC * 2 * KVW].rearrange("p (k n) -> p k n", k=NC))\
                .then_inc(setup_dve, 1)
            for b in range(B):
                dve.wait_ge(setup_mm, 3 + b)
                done(nc.vector.tensor_tensor(gamma[:, b].rearrange("p a c -> p (a c)"), ps[:, 2 + b, :],
                                             b_gamma_sb[:], ALU.add))
            dve.wait_ge(sm_ready, 1)
            dve.wait_ge(pads_set, 3)

            def layernorm(i, src, eps, step, to_pool, from_pool, ready):
                for t in range(NT):
                    last = nc.vector.bn_stats(stats[:, t, :], src(t))
                step(last)
                nc.vector.memset(wait_here[:], 0.0)
                for t in range(NT):
                    last = nc.vector.bn_aggr(mv[:, t, :], stats[:, t, :])
                step(last)
                nc.vector.tensor_scalar(var_eps[:], mv[:, :, 1], eps, None, ALU.add).then_inc(to_pool, 1)
                dve.wait_ge(from_pool, i + 1)
                for t in range(NT):
                    nc.vector.tensor_scalar(xn[:, t, :], src(t), mv[:, t, 0:1], rstd[:, t:t + 1],
                                            ALU.subtract, ALU.mult).then_inc(ready, 1)

            def put_stack(i, L, t, source, dst, hi2, lo_at):
                hi = dst(0)
                seq(i, nc.vector.tensor_copy(hi.bitcast(f32r), source))
                nc.vector.tensor_copy(dst(hi2), hi)
                return nc.vector.tensor_tensor(dst(lo_at), source, hi, ALU.subtract)

            def head_views(L, t, first, count, at):
                return stack[L][:, t, first:first + count, at * D:(at + 1) * D]

            def attention(i, L):
                src = (lambda t: x_in[:, t, :]) if L == 0 else (lambda t: x1[:, t, :])
                layernorm(i, src, LN0_EPS if L == 0 else LN1_EPS, lambda s: seq(i, s), var_ready[L],
                          rstd_ready[L], xn_ready[L])
                if L == 1:
                    for t in range(NT):
                        dve.wait_ge(proj_in_done[1], i * NT + t + 1)
                        nc.vector.tensor_tensor(vaug[1][:, t, :, 0:D],
                                                ps[:, 2 * t + 1, 0:C].rearrange("p (h d) -> p h d", d=D),
                                                qv_bias_sb[:, 1].rearrange("p (h d) -> p h d", d=D), ALU.add)
                        dve.wait_ge(k1_ready, i * NT + t + 1)
                        nc.vector.tensor_tensor(qk[:, t, 0:C], ps[:, 2 * t, 0:C], qv_bias_sb[:, 0],
                                                ALU.add).then_inc(q1_ready, 1)
                for t in range(NT):
                    if L == 0:
                        nh = H + HKV
                        dve.wait_ge(raw_ready, i * NT + t + 1)
                        xv = qk[:, t, 0:QK0].rearrange("p (h d) -> p h d", d=D)
                        av = qk_a[:, t, 0:QK0].rearrange("p (h d) -> p h d", d=D)
                        bv = qk_b[:, t, 0:QK0].rearrange("p (h d) -> p h d", d=D)
                        cos = rope[:, t, 0, :].unsqueeze(1).to_broadcast([P, nh, D])
                        nc.vector.tensor_tensor(av, xv, cos, ALU.mult)
                        for lo, hi in ((0, D // 2), (D // 2, 0)):
                            sin = rope[:, t, 1, lo:lo + D // 2].unsqueeze(1).to_broadcast([P, nh, D // 2])
                            last = nc.vector.tensor_tensor(bv[:, :, lo:lo + D // 2], xv[:, :, hi:hi + D // 2], sin,
                                                           ALU.mult)
                        seq(i, last)
                        seq(i, nc.vector.tensor_tensor(av, av, bv, ALU.add))
                        for a in range(2):
                            src_q = qk_a[:, t, 0:C].rearrange("p (g a r d) -> p g a r d", a=2, r=4, d=D)[:, :, a]
                            dst_q = stack[0][:, t, 0:H, :].rearrange("p (g r a) s -> p g r a s", a=2, r=4)[:, :, :, a, :]
                            seq(i, nc.vector.tensor_copy(dst_q[:, :, :, 0:D].bitcast(f32r), src_q))
                            nc.vector.tensor_copy(dst_q[:, :, :, 2 * D:3 * D], dst_q[:, :, :, 0:D])
                            nc.vector.tensor_tensor(dst_q[:, :, :, D:2 * D], src_q, dst_q[:, :, :, 0:D], ALU.subtract)
                        src_k = qk_a[:, t, C:QK0].rearrange("p (h d) -> p h d", d=D)
                        k_at = (0, H, HKV)
                    else:
                        dve.wait_ge(squares_ready, i * NT + t + 1)
                        seq(i, nc.vector.tensor_reduce(ss[:, t, :], qk_a[:, t, :].rearrange("p (h d) -> p h d", d=D),
                                                       AX.X, ALU.add))
                        nc.vector.tensor_scalar(ss_min[:, t, :], ss[:, t, :], 1e-24, None, ALU.max)\
                            .then_inc(ss_ready, 1)
                        dve.wait_ge(rs_ready, i * NT + t + 1)
                        seq(i, nc.vector.tensor_tensor(rs[:, t, 0:H], rs[:, t, 0:H], sm[:], ALU.mult))
                        seq(i, nc.vector.tensor_tensor(
                            qk_b[:, t, :].rearrange("p (h d) -> p h d", d=D),
                            qk[:, t, :].rearrange("p (h d) -> p h d", d=D),
                            rs[:, t, :].unsqueeze(2).to_broadcast([P, 2 * H, D]), ALU.mult))
                        src_q = qk_b[:, t, 0:C].rearrange("p (h d) -> p h d", d=D)
                        put_stack(i, 1, t, src_q, lambda at: head_views(1, t, 0, H, at), 2, 1)
                        src_k = qk_b[:, t, C:2 * C].rearrange("p (h d) -> p h d", d=D)
                        k_at = (1, H, H)
                    put_stack(i, L, t, src_k, lambda at: head_views(L, t, k_at[1], k_at[2], at), 1, 2)\
                        .then_inc(stack_ready[L], 1)
                for m in range(1, FILLS[L], 2):
                    dve.wait_ge(fill_done[L], i * FILLS[L] + m + 1)
                    nc.vector.tensor_copy(qkT[L][:, 2 * FILL_ORDER[L][m]:2 * FILL_ORDER[L][m] + 2, :],
                                          ps[:, FILL_BANK[L][m], :].rearrange("p (j t) -> p j t", j=2))\
                        .then_inc(fill_dve[L], 1)

                def maxima(g):
                    for u in range(S_USES[L]):
                        s = S_USES[L] * g + u
                        dve.wait_ge(s_done[L], i * S_USES[L] * NG + s + 1)
                        if L == 0 and u == 0:
                            heads, t, nh = GROUP * g, 0, GROUP
                        elif L == 0:
                            heads, t, nh = GROUP * g + 2 * (u - 1), 1, 2
                        else:
                            heads, t, nh = GROUP * g + 2 * (u // 2), u % 2, 2
                        nc.vector.tensor_reduce(negmax[:, heads:heads + nh, t],
                                                ps[:, SB + s % 2, :].rearrange("p (h k) -> p h k", h=nh),
                                                AX.X, ALU.max, negate=True).then_inc(max_done[L], 1)
                    dve.wait_ge(max_done[L], i * S_USES[L] * NG + S_USES[L] * (g + 1))
                    nm = negmax[:, GROUP * g:GROUP * (g + 1), :].rearrange("p h t -> p t h")
                    seq(i, nc.vector.tensor_copy(m_parts[:, g, :, :, 0].bitcast(f32r), nm))
                    nc.vector.tensor_tensor(m_parts[:, g, :, :, 1], nm, m_parts[:, g, :, :, 0],
                                            ALU.subtract).then_inc(m_ready[L], 1)

                def divide(g):
                    dve.wait_ge(otr_done[L], i * NG + g + 1)
                    ov = ps[:, MB, 0:2 * P].rearrange("p (t h s) -> p t h s", t=NT, h=GROUP)
                    seq(i, nc.vector.reciprocal(den[:], ov[:, :, :, D]))
                    for t in range(NT):
                        og = o[:, t, g * GROUP * D:(g + 1) * GROUP * D]
                        ogv, ovv = og.rearrange("p (h d) -> p h d", d=D), ov[:, t, :, 0:D]
                        dv = den[:, t, :].unsqueeze(2).to_broadcast([P, GROUP, D])
                        if L == 1:
                            ogv = og.rearrange("p (b a d) -> p a b d", a=2, d=D)
                            ovv = ovv.rearrange("p (a b) d -> p a b d", a=2)
                            dv = den[:, t, :].rearrange("p (a b) -> p a b", a=2).unsqueeze(3)\
                                .to_broadcast([P, 2, 2, D])
                        last = nc.vector.tensor_tensor(ogv, ovv, dv, ALU.mult)
                    last.then_inc(o_ready[L], 1)

                def evacuate(g):
                    dve.wait_ge(av_done[L], i * NG + g + 1)
                    nc.vector.tensor_copy(oT_raw[:], ps[:, OB, 0:T]).then_inc(oT_evac[L], 1)

                maxima(0)
                for g in range(NG):
                    if g + 1 < NG:
                        maxima(g + 1)
                    if g >= 2:
                        divide(g - 2)
                    if g >= 1:
                        evacuate(g - 1)
                divide(NG - 2)
                evacuate(NG - 1)
                divide(NG - 1)

            with dve.Fori(0, B) as i:
                n[0] = 0
                dve.wait_ge(x_loaded, i * 16 + 16)
                seq(i, nc.vector.tensor_copy(ada_now[:], adaT[:, :, i]))
                attention(i, 0)
                for t in range(NT):
                    dve.wait_ge(proj_done[0], i * NT + t + 1)
                    nc.vector.tensor_tensor(x1[:, t, :], x_in[:, t, :], ps[:, SB + t, 0:C],
                                            ALU.add).then_inc(x_ready[0], 1)
                dve.wait_ge(x_ready[0], i * NT + NT)
                attention(i, 1)
                dve.wait_ge(x1b_ready, i + 1)
                for t in range(NT):
                    dve.wait_ge(proj_done[1], i * NT + t + 1)
                    seq(i, nc.vector.tensor_tensor(scaled[:, t, :], ps[:, SB + t, 0:C], gamma[:, i, 0, :], ALU.mult))
                    nc.vector.tensor_tensor(x2[:, i, t, :], scaled[:, t, :], x1b[:, t, :],
                                            ALU.add).then_inc(x_ready[1], 1)
                assert n[0] == DVE_SEQ, n[0]

            LN2 = 2 + NT + 1
            with dve.Fori(0, B) as i:
                m = [0]

                def step(ins):
                    m[0] += 1
                    ins.then_inc(ln2_seq, 1)
                    dve.wait_ge(ln2_seq, i * LN2 + m[0])
                dve.wait_ge(x_ready[1], B * NT)
                step(nc.vector.tensor_copy(ada_now[:], adaT[:, :, i]))
                layernorm(i, lambda t: x2[:, i, t, :], LN1_EPS, step, var2_ready, rstd2_ready, xn2_ready)
                dve.wait_ge(x2b_ready, i + 1)
                for t in range(NT):
                    dve.wait_ge(fc2_done, i * NT + t + 1)
                    step(nc.vector.tensor_tensor(scaled[:, t, :], ps[:, SB + t, 0:C], gamma[:, i, 1, :], ALU.mult))
                    nc.vector.tensor_tensor(x2[:, i, t, :], scaled[:, t, :], x2b[:, t, :],
                                            ALU.add).then_inc(y_ready, 1)
                assert m[0] == LN2, m[0]

        @block.tensor
        def _(pe):
            mm, tr = nc.tensor.matmul, nc.tensor.transpose
            pe.wait_ge(cond_in, COND_IN)
            pe.wait_ge(silu_ready, 1)
            for a in range(NADA):
                for k in range(NC):
                    if a < ADA0:
                        w, rhs = w_ada_sb[:, k, a * P:(a + 1) * P], condT_sb[:, k, :]
                    else:
                        col = 2 * C + (a - ADA0) * P
                        w, rhs = w_ada1_sb[:, k, col:col + P], siluT[:, k, :]
                    last = mm(ps[:, 0, a * B:(a + 1) * B], w, rhs, start=k == 0, stop=k == NC - 1)
            last.then_inc(setup_mm, 1)
            pe.wait_ge(consts_in, CONSTS_IN)
            for k in range(NC):
                last = mm(ps[:, 1, k * 2 * KVW:(k + 1) * 2 * KVW], wkd_sb[:, k * P:(k + 1) * P], wkuv_sb[:],
                          start=True, stop=True)
            last.then_inc(setup_mm, 1)
            for b in range(B):
                for k in range(NC):
                    last = mm(ps[:, 2 + b, :], silu_b[:, k, b, :], w_ada1_sb[:, k, 0:2 * C],
                              start=k == 0, stop=k == NC - 1)
                last.then_inc(setup_mm, 1)
            pe.wait_ge(setup_dve, 7)
            pe.wait_ge(late_in, LATE_IN)
            pe.wait_ge(dve_setup, 12)

            def transposed_norm(i, ready, count):
                for t in range(NT):
                    pe.wait_ge(ready, i * NT + t + 1)
                    for c in range(NC):
                        last = tr(ps[:, MB, c * T + t * P:c * T + (t + 1) * P], xn[:, t, c * P:(c + 1) * P], ident[:])
                last.then_inc(count, 1)

            def scores(i, L, g):
                for u in range(S_USES[L]):
                    s = S_USES[L] * g + u
                    if s >= 2:
                        pe.wait_ge(max_done[L], i * S_USES[L] * NG + s - 1)
                    bank = ps[:, SB + s % 2, :]
                    if L == 0 and u == 0:
                        t, heads, keys = 0, range(GROUP * g, GROUP * g + GROUP), P
                    elif L == 0:
                        t, keys = 1, T
                        heads = range(GROUP * g + 2 * (u - 1), GROUP * g + 2 * u)
                    else:
                        t, keys = u % 2, T
                        heads = range(GROUP * g + 2 * (u // 2), GROUP * g + 2 * (u // 2) + 2)
                    nh = len(heads)
                    if L == 0:
                        hide = hide_q[:, 0:P] if t == 0 else hide_q[:, P:3 * P]
                        mm(bank, ident_b[:], hide.unsqueeze(1).to_broadcast([P, nh, keys]), start=True, stop=False)
                    else:
                        for j, part in enumerate((bias_hi, bias_lo)):
                            mm(bank, ident_r[:], part[:, 0, t, :].unsqueeze(1).to_broadcast([P, nh, keys]),
                               start=j == 0, stop=False)
                    for j, h in enumerate(heads):
                        qb, kb, half = place(L, h)
                        last = mm(bank[:, j * keys:(j + 1) * keys],
                                  qkT[L][half:half + STACK, qb, t * P:(t + 1) * P],
                                  qkT[L][half:half + STACK, kb, 0:keys], start=False, stop=j == nh - 1)
                    last.then_inc(s_done[L], 1)

            def place(L, h):
                h = head_at(L, h)
                if L == 0:
                    return (h // 8) * 4 + h % 4, H // 2 + h // 8, SLOT * ((h // 4) % 2)
                return h // 2, H // 2 + h // 2, SLOT * (h % 2)

            def transposed_maxima(i, L, g):
                pe.wait_ge(m_ready[L], i * NG + g + 1)
                if g >= 3:
                    pe.wait_ge(o_ready[L], i * NG + g - 2)
                for at, t in enumerate((0, 1, 1) if L == 0 else (0, 1)):
                    last = tr(ps[0:2 * GROUP, MB, at * P:(at + 1) * P],
                              m_parts[:, g, t].rearrange("p h a -> p (h a)"), ident[:])
                last.then_inc(mT_done[L], 1)

            def scores_T(i, L, g):
                pe.wait_ge(mT_ready[L], i * NG + g + 1)
                for p in range(2):
                    n = 2 * g + p
                    if n >= 2:
                        pe.wait_ge(exp_done[L], i * 2 * NG + n - 1)
                    for j in range(2):
                        h = GROUP * g + 2 * p + j
                        qb, kb, half = place(L, h)
                        bank = ps[:, TB + 2 * p + j, :]
                        if L == 0:
                            mm(bank[:, 0:3 * P], ident_b[:], hide_k[:], start=True, stop=False)
                            mm(bank[:, 0:3 * P], sel[:, 2 * p + j, :], mT[:, g % 2, :], start=False, stop=False)
                            spans = ((0, 0, 0, T), (1, T, P, T))
                        else:
                            for a, part in enumerate((bias_hi, bias_lo)):
                                mm(bank, ident_r[:], part[:, 1].rearrange("p t q -> p (t q)"),
                                   start=a == 0, stop=False)
                            mm(bank, sel[:, 2 * p + j, :], mT[:, g % 2, 0:T].unsqueeze(1).to_broadcast([2 * GROUP, 2, T]),
                               start=False, stop=False)
                            spans = ((0, 0, 0, T), (1, T, 0, T))
                        for kt, col, q0, q1 in spans:
                            last = mm(bank[:, col:col + q1 - q0], qkT[L][half:half + STACK, kb, kt * P:(kt + 1) * P],
                                      qkT[L][half:half + STACK, qb, q0:q1], start=False, stop=kt == 1)
                    last.then_inc(st_done[L], 1)

            def outputs(i, L, g):
                pe.wait_ge(exp_done[L], i * 2 * NG + 2 * g + 2)
                if g >= 1:
                    pe.wait_ge(oT_evac[L], i * NG + g)
                for kt in range(2):
                    q0 = P if L == 0 and kt == 1 else 0
                    for j in range(GROUP):
                        vh = g if L == 0 else head_at(L, GROUP * g + j)
                        last = mm(ps[2 * D * j:2 * D * (j + 1), OB, q0:T], vaug[L][:, kt, vh, :],
                                  prob[:, g % 2, j, kt * T:kt * T + T - q0], start=kt == 0, stop=kt == 1)
                last.then_inc(av_done[L], 1)

            def transposed_outputs(i, L, g):
                pe.wait_ge(oT_evac[L], i * NG + g + 1)
                pe.wait_ge(mT_ready[L], i * NG + min(g + 3, NG))
                if g >= 1:
                    pe.wait_ge(o_ready[L], i * NG + g)
                for t in range(NT):
                    last = tr(ps[:, MB, t * P:(t + 1) * P], oT_raw[:, t * P:(t + 1) * P], ident[:])
                last.then_inc(otr_done[L], 1)

            def attention(i, L):
                transposed_norm(i, xn_ready[L], xnT_done[L])
                pe.wait_ge(hT_ready[L], i * NC + NC)
                w = w0_sb if L == 0 else wqkv_sb
                for t in range(NT):
                    spans = ((SB + t, 0, W0),) if L == 0 else ((2 * t, 0, 2 * C), (2 * t + 1, 2 * C, 3 * C))
                    for bank, n0, n1 in spans:
                        for c in range(NC):
                            last = mm(ps[:, bank, 0:n1 - n0], hT[:, c, t * P:(t + 1) * P], w[:, c, n0:n1],
                                      start=c == 0, stop=c == NC - 1)
                    last.then_inc(proj_in_done[L], 1)
                pe.wait_ge(stack_ready[L], i * NT + NT)
                for n in range(FILLS[L]):
                    for j in range(2):
                        blk = 2 * FILL_ORDER[L][n] + j
                        for t in range(NT):
                            last = tr(ps[:, FILL_BANK[L][n], j * T + t * P:j * T + (t + 1) * P],
                                      stack[L][:, t, 2 * blk:2 * blk + 2, :].rearrange("p h s -> p (h s)"), ident[:])
                    last.then_inc(fill_done[L], 1)
                pe.wait_ge(fill_act[L], (i + 1) * ((FILLS[L] + 1) // 2))
                pe.wait_ge(fill_dve[L], (i + 1) * (FILLS[L] // 2))
                scores(i, L, 0)
                for g in range(NG):
                    if g + 1 < NG:
                        scores(i, L, g + 1)
                    transposed_maxima(i, L, g)
                    if g >= 2:
                        transposed_outputs(i, L, g - 2)
                    scores_T(i, L, g)
                    if g >= 1:
                        outputs(i, L, g - 1)
                transposed_outputs(i, L, NG - 2)
                outputs(i, L, NG - 1)
                transposed_outputs(i, L, NG - 1)
                pe.wait_ge(o_ready[L], i * NG + NG)
                for c in range(NC):
                    for t in range(NT):
                        last = tr(ps[:, MB, c * T + t * P:c * T + (t + 1) * P], o[:, t, c * P:(c + 1) * P], ident[:])
                last.then_inc(oc_done[L], 1)
                pe.wait_ge(oc_ready[L], i + 1)
                w = wo_sb if L == 0 else wproj_sb
                for t in range(NT):
                    for c in range(NC):
                        last = mm(ps[:, SB + t, 0:C], oT[:, c, t * P:(t + 1) * P], w[:, c, :],
                                  start=c == 0, stop=c == NC - 1)
                    last.then_inc(proj_done[L], 1)

            with pe.Fori(0, B) as i:
                attention(i, 0)
                attention(i, 1)

            with pe.Fori(0, B) as i:
                transposed_norm(i, xn2_ready, xn2T_done)
                pe.wait_ge(h2T_ready, i * NC + NC)
                for f in range(NF):
                    if f >= 4:
                        pe.wait_ge(gelu_done, i * NF + f - 3)
                    for c in range(NC):
                        last = mm(ps[:, 2 + f % 4, 0:T], wfc1_sb[:, c, f * P:(f + 1) * P], hT[:, c, :],
                                  start=c == 0, stop=c == NC - 1)
                    last.then_inc(fc1_done, 1)
                for t in range(NT):
                    for f in range(NF):
                        if t == 0:
                            pe.wait_ge(gelu_done, i * NF + f + 1)
                        last = mm(ps[:, SB + t, 0:C], gT[:, f, t * P:(t + 1) * P], wfc2_sb[:, f, :],
                                  start=f == 0, stop=f == NF - 1)
                    last.then_inc(fc2_done, 1)


def head_at(L, n):
    return n if L == 0 else n // GROUP * GROUP + (0, 2, 1, 3)[n % GROUP]


FILL_ORDER = ((4, 0, 1, 2, 3), (0, 4, 1, 5, 2, 6, 3, 7))
FILL_BANK = ((2, 3, 4, 5, 6), (0, 1, 2, 3, 4, 5, 6, 7))


def kernel(x, cond_2048, mask_1x1xSxS_ff0, L0_cond_W_ada, L0_cond_b_ada, L0_cond_Wq, L0_cond_Wkd, L0_cond_Wku,
           L0_cond_Wvu, L0_cond_Wo, L1_cond_Wqkv, L1_cond_q_bias, L1_cond_v_bias, L1_cond_scale_mul_log,
           L1_cond_Wproj, L1_cond_bproj, L1_cond_Wada, L1_cond_bada, L1_cond_Wfc1, L1_cond_bfc1, L1_cond_Wfc2,
           L1_cond_bfc2):
    import numpy as np
    import concourse.bacc as bacc
    from concourse.bass_utils import run_bass_kernel_spmd

    def arr(a):
        return np.ascontiguousarray(np.asarray(a))

    pos = np.arange(T)
    freqs = (1.0 / np.float32(10000.0) ** (np.arange(0, D, 2, dtype=np.float32) / D)).astype(np.float32)
    angle = pos.astype(np.float32)[:, None] * freqs[None, :]
    rope = np.zeros((T, 2, D), np.float32)
    rope[:, 0, :] = np.concatenate([np.cos(angle), np.cos(angle)], -1)
    rope[:, 1, :] = np.concatenate([-np.sin(angle), np.sin(angle)], -1)
    blk = pos // 128
    hidden = ((np.abs(pos[None, :] - pos[:, None]) > 32) & ~(pos % 64 == 0)[None, :]) | (blk[None, :] > blk[:, None])
    hide = np.where(hidden, np.float32(NEG), np.float32(0.0)).astype(np.float32)
    hide_q = np.concatenate([hide[0:P, 0:P], hide[P:T, :]], 1)
    hide_k = np.concatenate([hide.T[0:P, :], hide.T[P:T, P:T]], 1)
    sel = np.zeros((2 * GROUP, GROUP, P), np.float32)
    for j in range(GROUP):
        sel[2 * j:2 * j + 2, j, :] = 1.0

    bada, wada = arr(L1_cond_bada), arr(L1_cond_Wada)
    mask = arr(mask_1x1xSxS_ff0).reshape(T, T)
    arrays = {
        "x": arr(x),
        "condT": arr(arr(cond_2048).T),
        "w_adaT": arr(arr(L0_cond_W_ada).T),
        "w_ada1T": arr(wada.T),
        "b_adaT": arr(np.concatenate([arr(L0_cond_b_ada), bada[2 * C:]]).reshape(NADA, P).T),
        "b_gamma": bada[0:2 * C],
        "wqT": arr(arr(L0_cond_Wq).T),
        "wkd": arr(L0_cond_Wkd),
        "wkuvT": arr(np.concatenate([arr(L0_cond_Wku), arr(L0_cond_Wvu)], 0).T),
        "woT": arr(arr(L0_cond_Wo).T),
        "wqkvT": arr(arr(L1_cond_Wqkv).T),
        "q_bias": arr(L1_cond_q_bias),
        "v_bias": arr(L1_cond_v_bias),
        "scale_log": arr(L1_cond_scale_mul_log).reshape(H),
        "wprojT": arr(arr(L1_cond_Wproj).T),
        "bproj": arr(L1_cond_bproj),
        "wfc1T": arr(arr(L1_cond_Wfc1).T),
        "bfc1T": arr(arr(L1_cond_bfc1).reshape(NF, P).T),
        "wfc2T": arr(arr(L1_cond_Wfc2).T),
        "bfc2": arr(L1_cond_bfc2),
        "bias_q": mask,
        "bias_k": arr(mask.T),
        "ident_d": np.eye(P, dtype=np.float32),
        "rope_d": rope,
        "hide_q_d": arr(hide_q),
        "hide_k_d": arr(hide_k),
        "sel_d": sel,
    }
    nc = bacc.Bacc("TRN2", target_bir_lowering=False, num_devices=1)
    aps = {n: nc.dram_tensor("in_" + n, a.shape, mybir.dt.from_np(a.dtype), kind="ExternalInput").ap()
           for n, a in arrays.items()}
    out = nc.dram_tensor("out_0", (B, T, C), mybir.dt.float32, kind="ExternalOutput").ap()
    build(nc, out=out, **aps)
    r = run_bass_kernel_spmd(nc, [{"in_" + n: a for n, a in arrays.items()}], core_ids=[0])
    return r.results[0]["out_0"]
```

```python
import concourse.bass as bass
from concourse import mybir
from contextlib import ExitStack

B, T, C = 4, 256, 256
P = 128
NT, NC = T // P, C // P
H, D, HKV = 16, 16, 4
GROUP = 4
NG = H // GROUP
HID = 4 * C
NF = HID // P
SLOT = 64
STACK = 3 * D
KVW = HKV * D
QK0 = C + KVW
W0 = C + 2 * KVW
NEG = -1e30
LOWEST = -3e38
LN0_EPS, LN1_EPS = 1e-5, 1e-6
ADA0, ADA1 = 4, 8
NADA = ADA0 + ADA1

SB = 0
TB, NTB = 2, 3
OB = 5
MB = 6
XB = 7

S_USES = (3, 4)
S_ALL = (S_USES[0] * NG, S_USES[1] * NG)
FILL_ORDER = ((4, 0, 1, 2, 3), (0, 4, 1, 5, 2, 6, 3, 7))
FILL_BANK = ((7, 0, 1, 2, 3), (7, 0, 1, 2, 3, 4, 0, 1))
FILL_DVE = ((2, 4), (2, 4, 6))
FILLS = (5, 8)
N_DVE = (len(FILL_DVE[0]), len(FILL_DVE[1]))
N_ACT = (FILLS[0] - N_DVE[0], FILLS[1] - N_DVE[1])
QKV_USES = (2, 3)
GB = (2, 3, 4, 6)
SEQ_A, SEQ_F, SEQ_P = (7, 7), (1, 2), (13, 25, 3)


def build(nc, x, condT, w_adaT, w_ada1T, b_adaT, b_gamma, wqT, wkd, wkuvT, woT, wqkvT, q_bias, v_bias,
          scale_log, wprojT, bproj, wfc1T, bfc1T, wfc2T, bfc2, bias_q, bias_k, ident_d, rope_d, hide_q_d,
          hide_k_d, sel_d, out):
    f32, f32r, bf16 = mybir.dt.float32, mybir.dt.float32r, mybir.dt.bfloat16
    ALU, ACT, AX = mybir.AluOpType, mybir.ActivationFunctionType, mybir.AxisListType

    ctx = ExitStack()
    with ctx:
        def sb(name, shape, dt=f32):
            return ctx.enter_context(nc.sbuf_tensor(name, shape, dt))

        def sem(name):
            return ctx.enter_context(nc.semaphore(name))

        condT_sb = sb("condT_sb", [P, NC, B])
        w_ada_sb = sb("w_ada_sb", [P, NC, 2 * C])
        w_ada1_sb = sb("w_ada1_sb", [P, NC, 6 * C])
        b_ada_sb = sb("b_ada_sb", [P, NADA])
        b_gamma_sb = sb("b_gamma_sb", [P, 2 * C])
        w0_sb = sb("w0_sb", [P, NC, W0])
        wkd_sb = sb("wkd_sb", [64, C])
        wkuv_sb = sb("wkuv_sb", [64, 2 * KVW])
        wo_sb = sb("wo_sb", [P, NC, C])
        wqkv_sb = sb("wqkv_sb", [P, NC, 3 * C])
        wproj_sb = sb("wproj_sb", [P, NC, C])
        wfc1_sb = sb("wfc1_sb", [P, NC, HID])
        wfc2_sb = sb("wfc2_sb", [P, NF, C])
        bfc1_sb = sb("bfc1_sb", [P, NF])
        qv_bias_sb = sb("qv_bias_sb", [P, 2, C])
        out_bias_sb = sb("out_bias_sb", [P, 2, C])
        scale_sb = sb("scale_sb", [P, H])
        ident = sb("ident", [P, P])
        ident_b = sb("ident_b", [P, P], bf16)
        ident_r = sb("ident_r", [P, P], f32r)
        rope = sb("rope", [P, NT, 2, D])
        hide_f = sb("hide_f", [P, 2, 384])
        hide_q = sb("hide_q", [P, 384], bf16)
        hide_k = sb("hide_k", [P, 384], bf16)
        sel_f = sb("sel_f", [2 * GROUP, GROUP, P])
        sel = sb("sel", [2 * GROUP, GROUP, P], f32r)
        bias_f = sb("bias_f", [P, 2, NT, T])
        bias_hi = sb("bias_hi", [P, 2, NT, T], f32r)
        bias_lo = sb("bias_lo", [P, 2, NT, T], f32r)
        biased_f = sb("biased_f", [P, 2, NT, T])
        biased_rows = sb("biased_rows", [P, 1])
        ones = sb("ones", [P, 1])
        biased_flag = sb("biased_flag", [1, 1], mybir.dt.int32)
        silu_e = sb("silu_e", [P, NC, B])
        silu_d = sb("silu_d", [P, NC, B])
        silu_r = sb("silu_r", [P, NC, B])
        siluT = sb("siluT", [P, NC, B])
        silu_b = sb("silu_b", [P, NC, B, P])
        adaT = sb("adaT", [P, NADA, B])
        gamma = sb("gamma", [P, B, 2, C])
        sm_l = sb("sm_l", [P, H])
        sm = sb("sm", [P, H])
        xs = sb("xs", [P, B, NT, C])
        bg = sb("bg", [P, B, 2, C])
        ada_now = sb("ada_now", [P, NADA])
        stats = sb("stats", [P, NT, 6])
        mv = sb("mv", [P, NT, 2])
        wait_here = sb("wait_here", [P, 1])
        var_eps = sb("var_eps", [P, NT])
        rstd = sb("rstd", [P, NT])
        minus_half = sb("minus_half", [P, NT])
        xn = sb("xn", [P, NT, C])
        hT = sb("hT", [P, NC, T])
        qk = sb("qk", [P, NT, 2 * C])
        qk_a = sb("qk_a", [P, NT, 2 * C])
        qk_b = sb("qk_b", [P, NT, 2 * C])
        ss = sb("ss", [P, NT, 2 * H])
        nt_a = sb("nt_a", [P, NT, 2 * H])
        nt_b = sb("nt_b", [P, NT, 2 * H])
        rs = sb("rs", [P, NT, 2 * H])
        stack1 = sb("stack1", [P, NT, 2 * H, SLOT])
        stack = [stack1[:, :, 0:H + HKV, :], stack1[:]]
        qkT1 = sb("qkT1", [P, H, T], f32r)
        qkT = [qkT1[:, 0:(H + HKV) // 2, :], qkT1[:]]
        vaug = [sb("vaug0", [P, NT, HKV, 2 * D]), sb("vaug1", [P, NT, H, 2 * D])]
        vraw = sb("vraw", [P, NT, C])
        negmax = sb("negmax", [P, H, NT])
        m_parts = sb("m_parts", [P, NG, NT, GROUP, 2])
        mT = sb("mT", [2 * GROUP, 2, 3 * P], f32r)
        prob = sb("prob", [P, 2, GROUP, 2 * T])
        oT_raw = sb("oT_raw", [P, 2, T])
        den = sb("den", [P, NT, GROUP])
        o = sb("o", [P, NT, C])
        oT = sb("oT", [P, NC, T])
        scaled = sb("scaled", [P, NT, C])
        gT = prob[:].rearrange("p a h q -> p (a h q)")[:, 0:NF * T].rearrange("p (f q) -> p f q", f=NF)
        ps = ctx.enter_context(nc.psum_tensor("ps", [P, 8, 512], f32))

        cond_in, consts_in, late_in = sem("cond_in"), sem("consts_in"), sem("late_in")
        silu_exp, silu_ready, sm_ready = sem("silu_exp"), sem("silu_ready"), sem("sm_ready")
        dve_setup, sm_min = sem("dve_setup"), sem("sm_min")
        setup_mm, setup_dve, pads_set = sem("setup_mm"), sem("setup_dve"), sem("pads_set")
        rows_counted, count_done, flag_ready = sem("rows_counted"), sem("count_done"), sem("flag_ready")
        x_first, x_rest = sem("x_first"), sem("x_rest")

        def per_layer(name, n=2):
            return [sem(f"{name}{L}") for L in range(n)]
        pre_seq, xn_ready, xnT_done = per_layer("pre_seq", 3), per_layer("xn_ready", 3), per_layer("xnT_done", 3)
        var_ready, rstd_ready, hT_ready = per_layer("var_ready", 3), per_layer("rstd_ready", 3), per_layer("hT_ready", 3)
        qkv_done, raw_ready, v_ready = per_layer("qkv_done"), per_layer("raw_ready"), per_layer("v_ready")
        biased_ready, stack_ready = sem("biased_ready"), per_layer("stack_ready")
        fill_done, fill_act, fill_dve = per_layer("fill_done"), per_layer("fill_act"), per_layer("fill_dve")
        att_seq, fin_seq = per_layer("att_seq"), per_layer("fin_seq")
        s_done, max_done, m_ready = per_layer("s_done"), per_layer("max_done"), per_layer("m_ready")
        mT_done, mT_ready = per_layer("mT_done"), per_layer("mT_ready")
        st_done, exp_done, av_done = per_layer("st_done"), per_layer("exp_done"), per_layer("av_done")
        oT_evac, otr_done, o_ready = per_layer("oT_evac"), per_layer("otr_done"), per_layer("o_ready")
        oc_done, oc_ready = per_layer("oc_done"), per_layer("oc_ready")
        proj_done, x_ready = per_layer("proj_done"), per_layer("x_ready")
        bg_ready, xb_ready, scaled_ready = sem("bg_ready"), per_layer("xb_ready", 3), per_layer("scaled_ready", 3)
        fc1_done, gelu_done, fc2_done = sem("fc1_done"), sem("gelu_done"), sem("fc2_done")
        y_ready, y_stored = sem("y_ready"), sem("y_stored")

        COND_IN, CONSTS_IN, LATE_IN = 5 * 16, 11 * 16, 11 * 16
        block = ctx.enter_context(nc.Block())

        x_v = x.rearrange("b (t p) c -> b p t c", p=P)
        out_v = out.rearrange("b (t p) c -> b p t c", p=P)

        def wide(w):
            return w.rearrange("(k p) n -> p k n", p=P)

        def rows(v):
            return v.partition_broadcast(P)

        @block.sync
        def _(sp):
            sp.dma_start(condT_sb[:], condT.rearrange("(k p) b -> p k b", p=P)).then_inc(cond_in, 16)
            sp.dma_start(xs[:, 0], x_v[0]).then_inc(x_first, 16)
            sp.dma_start(ident[:], ident_d).then_inc(consts_in, 16)
            sp.dma_start(w_ada_sb[:], wide(w_adaT)).then_inc(cond_in, 16)
            sp.dma_start(w_ada1_sb[:], wide(w_ada1T)).then_inc(cond_in, 16)
            sp.dma_start(b_ada_sb[:], b_adaT).then_inc(cond_in, 16)
            sp.dma_start(b_gamma_sb[:], rows(b_gamma)).then_inc(cond_in, 16)
            sp.dma_start(wkd_sb[:], wkd).then_inc(consts_in, 16)
            sp.dma_start(wkuv_sb[:], wkuvT).then_inc(consts_in, 16)
            sp.dma_start(w0_sb[:, :, 0:C], wide(wqT)).then_inc(consts_in, 16)
            sp.dma_start(rope[:], rope_d.rearrange("(t p) a d -> p t a d", p=P)).then_inc(consts_in, 16)
            sp.dma_start(hide_f[:, 0, :], hide_q_d).then_inc(consts_in, 16)
            sp.dma_start(hide_f[:, 1, :], hide_k_d).then_inc(consts_in, 16)
            sp.dma_start(sel_f[:], sel_d).then_inc(consts_in, 16)
            sp.dma_start(wo_sb[:], wide(woT)).then_inc(consts_in, 16)
            sp.dma_start(bias_f[:, 0], bias_q.rearrange("(t p) k -> p t k", p=P)).then_inc(consts_in, 16)
            sp.dma_start(bias_f[:, 1], bias_k.rearrange("(t p) k -> p t k", p=P)).then_inc(consts_in, 16)
            sp.dma_start(xs[:, 1:B].rearrange("p b t c -> p (b t) c"),
                         x[1:B].rearrange("b (t p) c -> p (b t) c", p=P)).then_inc(x_rest, 16)
            with sp.Fori(0, B) as i:
                sp.wait_ge(y_ready, i * NT + NT)
                sp.dma_start(out_v[i], xs[:, i]).then_inc(y_stored, 16)
            sp.wait_ge(y_stored, B * 16)

        @block.gpsimd
        def _(pool):
            pool.memset(stack1[:, :, :, STACK:SLOT], 0.0).then_inc(pads_set, 1)
            for v in vaug:
                pool.memset(v[:, :, :, D:2 * D], 1.0).then_inc(pads_set, 1)
            pool.memset(minus_half[:], -0.5).then_inc(pads_set, 1)
            pool.wait_ge(pads_set, 4)

            def prepare(u, L, before=None):
                pool.wait_ge(var_ready[L], u + 1)
                pool.tensor_tensor(rstd[:], var_eps[:], minus_half[:], ALU.pow).then_inc(rstd_ready[L], 1)
                if L > 0:
                    pool.wait_ge(xn_ready[L], u * NT + NT)
                    pool.tensor_tensor(xs[:, u], xs[:, u], bg[:, u, L - 1].unsqueeze(1).to_broadcast([P, NT, C]),
                                       ALU.add).then_inc(xb_ready[L], 1)
                if L == 1:
                    for t in range(NT):
                        pool.wait_ge(raw_ready[1], u * QKV_USES[1] + t + 1)
                        pool.tensor_tensor(qk[:, t, 0:C], qk[:, t, 0:C], qv_bias_sb[:, 0], ALU.add)\
                            .then_inc(biased_ready, 1)
                if L < 2:
                    pool.wait_ge(raw_ready[L], (u + 1) * QKV_USES[L])
                    if before is not None:
                        pool.wait_ge(av_done[before[0]], (before[1] + 1) * NG)
                    if L == 0:
                        v = vraw[:, :, 0:KVW].rearrange("p t (h d) -> p t h d", d=D)
                        pool.tensor_tensor(vaug[0][:, :, :, 0:D], v, vaug[0][:, :, :, D:2 * D], ALU.mult).then_inc(v_ready[0], 1)
                    else:
                        pool.tensor_tensor(vaug[1][:, :, :, 0:D], vraw[:].rearrange("p t (h d) -> p t h d", d=D),
                                           qv_bias_sb[:, 1].rearrange("p (h d) -> p h d", d=D).unsqueeze(1)
                                           .to_broadcast([P, NT, H, D]), ALU.add).then_inc(v_ready[1], 1)

            prepare(0, 0)
            pool.wait_ge(late_in, LATE_IN)
            pool.wait_ge(dve_setup, 13)
            for b in range(B):
                pool.tensor_tensor(bg[:, b], out_bias_sb[:], gamma[:, b], ALU.mult).then_inc(bg_ready, 1)
            with pool.Fori(0, B - 1) as i:
                prepare(i + 1, 0, (0, i))
            pool.wait_ge(bg_ready, B)
            prepare(0, 1, (0, B - 1))
            with pool.Fori(0, B - 1) as i:
                prepare(i + 1, 1, (1, i))
            prepare(0, 2)
            with pool.Fori(0, B - 1) as i:
                prepare(i + 1, 2)

        @block.scalar
        def _(act):
            act.dma_start(scale_sb[:], rows(scale_log)).then_inc(late_in, 16)
            act.dma_start(wqkv_sb[:, 0, :], wqkvT[0:P, :]).then_inc(late_in, 16)
            act.dma_start(wqkv_sb[:, 1, :], wqkvT[P:C, :]).then_inc(late_in, 16)
            act.dma_start(qv_bias_sb[:, 0], rows(q_bias)).then_inc(late_in, 16)
            act.dma_start(qv_bias_sb[:, 1], rows(v_bias)).then_inc(late_in, 16)
            act.dma_start(out_bias_sb[:, 0], rows(bproj)).then_inc(late_in, 16)
            act.dma_start(out_bias_sb[:, 1], rows(bfc2)).then_inc(late_in, 16)
            act.dma_start(wproj_sb[:], wide(wprojT)).then_inc(late_in, 16)
            act.dma_start(bfc1_sb[:], bfc1T).then_inc(late_in, 16)
            act.dma_start(wfc1_sb[:], wide(wfc1T)).then_inc(late_in, 16)
            act.dma_start(wfc2_sb[:], wide(wfc2T)).then_inc(late_in, 16)
            act.wait_ge(cond_in, COND_IN)
            nc.scalar.activation(silu_e[:], condT_sb[:], ACT.Exp, scale=-1.0).then_inc(silu_exp, 1)
            act.wait_ge(sm_min, 1)
            nc.scalar.activation(sm[:], sm_l[:], ACT.Exp).then_inc(sm_ready, 1)

            def modulate(u, L):
                act.wait_ge(xnT_done[L], u + 1)
                at_scale = (0, ADA0, ADA0 + 2)[L]
                at_shift = (2, ADA0 + 4, ADA0 + 6)[L]
                for c in range(NC):
                    nc.scalar.activation(hT[:, c, :], ps[:, XB, c * T:(c + 1) * T], ACT.Identity,
                                         bias=ada_now[:, at_shift + c:at_shift + c + 1],
                                         scale=ada_now[:, at_scale + c:at_scale + c + 1]).then_inc(hT_ready[L], 1)

            def take_qkv(u, L, n):
                act.wait_ge(qkv_done[L], u * QKV_USES[L] + n + 1)
                if L == 0:
                    nc.scalar.activation(vraw[:, n, 0:KVW], ps[:, XB, QK0:W0], ACT.Copy)
                    ins = nc.scalar.activation(qk[:, n, 0:QK0], ps[:, XB, 0:QK0], ACT.Copy)
                elif n < NT:
                    ins = nc.scalar.activation(qk[:, n, :], ps[:, XB, :], ACT.Copy)
                else:
                    ins = nc.scalar.activation(vraw[:].rearrange("p t c -> p (t c)"), ps[:, XB, :], ACT.Copy)
                ins.then_inc(raw_ready[L], 1)

            def take_fills(u, L, fills):
                for n in fills:
                    if n not in FILL_DVE[L]:
                        blk = 2 * FILL_ORDER[L][n]
                        act.wait_ge(fill_done[L], u * FILLS[L] + n + 1)
                        nc.scalar.activation(qkT[L][:, blk:blk + 2, :].rearrange("p j t -> p (j t)"),
                                             ps[:, FILL_BANK[L][n], :], ACT.Copy).then_inc(fill_act[L], 1)

            def prepare(u, L):
                modulate(u, L)
                for n in range(QKV_USES[L]):
                    take_qkv(u, L, n)
                take_fills(u, L, range(FILLS[L]))

            def take_projected(i, L):
                act.wait_ge(oc_done[L], i + 1)
                nc.scalar.activation(oT[:].rearrange("p c t -> p (c t)"), ps[:, MB, :],
                                     ACT.Copy).then_inc(oc_ready[L], 1)

            def attention(i, L, before, u, LN):
                cols = 3 * P if L == 0 else 2 * T
                width = 3 * P if L == 0 else T
                if before is not None:
                    take_projected(before[1], before[0])
                for g in range(NG):
                    act.wait_ge(mT_done[L], i * NG + g + 1)
                    nc.scalar.activation(mT[:, g % 2, 0:width], ps[0:2 * GROUP, MB, 0:width],
                                         ACT.Copy).then_inc(mT_ready[L], 1)
                    if g >= 1 and LN < 2 and g <= QKV_USES[LN]:
                        take_qkv(u, LN, g - 1)
                    for j in range(GROUP):
                        n = GROUP * g + j
                        if j == 0 and g >= 2:
                            act.wait_ge(av_done[L], i * NG + g - 1)
                        act.wait_ge(st_done[L], i * H + n + 1)
                        nc.scalar.activation(prob[:, g % 2, j, 0:cols], ps[:, TB + n % NTB, 0:cols], ACT.Exp,
                                             scale=D ** -0.5 if L == 0 else 1.0).then_inc(exp_done[L], 1)
                    if g == 0:
                        modulate(u, LN)
                    else:
                        take_outputs(i, L, g - 1)
                if LN < 2:
                    take_fills(u, LN, range(0, 3))
                take_outputs(i, L, NG - 1)
                if LN < 2:
                    take_fills(u, LN, range(3, FILLS[LN]))

            def take_outputs(i, L, g):
                act.wait_ge(av_done[L], i * NG + g + 1)
                nc.scalar.activation(oT_raw[:, g % 2, :], ps[:, OB, 0:T], ACT.Copy).then_inc(oT_evac[L], 1)

            def mlp(i, last):
                for f in range(NF):
                    act.wait_ge(fc1_done, i * NF + f + 1)
                    nc.scalar.activation(gT[:, f, :], ps[:, GB[f % len(GB)], 0:T], ACT.Gelu_apprx_tanh,
                                         bias=bfc1_sb[:, f:f + 1]).then_inc(gelu_done, 1)
                if not last:
                    modulate(i + 1, 2)

            prepare(0, 0)
            attention(0, 0, None, 1, 0)
            with act.Fori(1, B - 1) as i:
                attention(i, 0, (0, i - 1), i + 1, 0)
            attention(B - 1, 0, (0, B - 2), 0, 1)
            attention(0, 1, (0, B - 1), 1, 1)
            with act.Fori(1, B - 1) as i:
                attention(i, 1, (1, i - 1), i + 1, 1)
            attention(B - 1, 1, (1, B - 2), 0, 2)
            take_projected(B - 1, 1)
            with act.Fori(0, B - 1) as i:
                mlp(i, False)
            mlp(B - 1, True)

        @block.vector
        def _(dve):
            def chain(sem, u, per):
                n = [0]

                def step(ins):
                    n[0] += 1
                    ins.then_inc(sem, 1)
                    dve.wait_ge(sem, u * per + n[0])

                def finish():
                    assert n[0] == per, (sem, n[0], per)
                return step, finish

            setup = [0]

            def done(ins):
                setup[0] += 1
                ins.then_inc(dve_setup, 1)
                dve.wait_ge(dve_setup, setup[0])

            dve.wait_ge(silu_exp, 1)
            done(nc.vector.tensor_scalar(silu_d[:], silu_e[:], 1.0, None, ALU.add))
            done(nc.vector.reciprocal(silu_r[:], silu_d[:]))
            done(nc.vector.tensor_tensor(siluT[:], condT_sb[:], silu_r[:], ALU.mult))
            nc.vector.tensor_copy(silu_b[:], siluT[:].unsqueeze(3).to_broadcast([P, NC, B, P])).then_inc(silu_ready, 1)
            dve.wait_ge(consts_in, CONSTS_IN)
            nc.vector.tensor_copy(ident_b[:], ident[:]).then_inc(setup_dve, 1)
            nc.vector.tensor_copy(ident_r[:], ident[:]).then_inc(setup_dve, 1)
            nc.vector.tensor_copy(hide_q[:], hide_f[:, 0, :]).then_inc(setup_dve, 1)
            nc.vector.tensor_copy(hide_k[:], hide_f[:, 1, :]).then_inc(setup_dve, 1)
            nc.vector.tensor_copy(sel[:], sel_f[:]).then_inc(setup_dve, 1)
            done(nc.vector.tensor_scalar(bias_f[:], bias_f[:], LOWEST, None, ALU.max))
            done(nc.vector.tensor_copy(bias_hi[:], bias_f[:]))
            nc.vector.tensor_tensor(bias_lo[:], bias_f[:], bias_hi[:].bitcast(f32), ALU.subtract).then_inc(setup_dve, 1)
            nc.vector.memset(ones[:], 1.0)
            done(nc.vector.tensor_scalar(biased_f[:], bias_f[:], 0.0, None, ALU.not_equal))
            nc.vector.tensor_reduce(biased_rows[:], biased_f[:].rearrange("p a t k -> p (a t k)"), AX.X,
                                    ALU.add).then_inc(rows_counted, 1)
            dve.wait_ge(late_in, LATE_IN)
            nc.vector.tensor_scalar(sm_l[:], scale_sb[:], 4.605170185988092, None, ALU.min).then_inc(sm_min, 1)
            dve.wait_ge(setup_mm, 1)
            done(nc.vector.tensor_tensor(adaT[:], ps[:, 0, 0:NADA * B].rearrange("p (a b) -> p a b", b=B),
                                         b_ada_sb[:].unsqueeze(2).to_broadcast([P, NADA, B]), ALU.add))
            for first, count in ((0, 2), (ADA0, 4)):
                done(nc.vector.tensor_scalar(adaT[:, first:first + count, :], adaT[:, first:first + count, :],
                                             1.0, None, ALU.add))
            dve.wait_ge(setup_mm, 2)
            nc.vector.tensor_copy(w0_sb[:, :, C:W0], ps[:, 1, 0:NC * 2 * KVW].rearrange("p (k n) -> p k n", k=NC))\
                .then_inc(setup_dve, 1)
            for b in range(B):
                dve.wait_ge(setup_mm, 3 + b)
                done(nc.vector.tensor_tensor(gamma[:, b].rearrange("p a c -> p (a c)"), ps[:, 2 + b, :],
                                             b_gamma_sb[:], ALU.add))
            dve.wait_ge(count_done, 1)
            nc.vector.tensor_scalar(biased_flag[:], ps[0:1, 6, 0:1], 1.0, None, ALU.min).then_inc(flag_ready, 1)
            dve.wait_ge(sm_ready, 1)
            dve.wait_ge(pads_set, 4)

            def norm_stats(u, L, step):
                if L == 2 and not isinstance(u, int):
                    dve.wait_ge(hT_ready[2], u * NC)
                step(nc.vector.tensor_copy(ada_now[:], adaT[:, :, u]))
                if L > 0:
                    dve.wait_ge(x_ready[L - 1], u * NT + NT)
                for t in range(NT):
                    last = nc.vector.bn_stats(stats[:, t, :], xs[:, u, t, :])
                step(last)
                nc.vector.memset(wait_here[:], 0.0)
                for t in range(NT):
                    last = nc.vector.bn_aggr(mv[:, t, :], stats[:, t, :])
                step(last)
                nc.vector.tensor_scalar(var_eps[:], mv[:, :, 1], LN0_EPS if L == 0 else LN1_EPS, None,
                                        ALU.add).then_inc(var_ready[L], 1)

            def norm_apply(u, L):
                dve.wait_ge(rstd_ready[L], u + 1)
                for t in range(NT):
                    nc.vector.tensor_scalar(xn[:, t, :], xs[:, u, t, :], mv[:, t, 0:1], rstd[:, t:t + 1],
                                            ALU.subtract, ALU.mult).then_inc(xn_ready[L], 1)

            def put_stack(step, source, dst, hi2, lo_at):
                hi = dst(0)
                step(nc.vector.tensor_copy(hi.bitcast(f32r), source))
                nc.vector.tensor_copy(dst(hi2), hi)
                return nc.vector.tensor_tensor(dst(lo_at), source, hi, ALU.subtract)

            def slots(L, t, first, count):
                return lambda at: stack[L][:, t, first:first + count, at * D:(at + 1) * D]

            def rope_stack(u, t, step):
                nh = H + HKV
                dve.wait_ge(raw_ready[0], u * QKV_USES[0] + t + 1)
                xv = qk[:, t, 0:QK0].rearrange("p (h d) -> p h d", d=D)
                av = qk_a[:, t, 0:QK0].rearrange("p (h d) -> p h d", d=D)
                bv = qk_b[:, t, 0:QK0].rearrange("p (h d) -> p h d", d=D)
                cos = rope[:, t, 0, :].unsqueeze(1).to_broadcast([P, nh, D])
                nc.vector.tensor_tensor(av, xv, cos, ALU.mult)
                for lo, hi in ((0, D // 2), (D // 2, 0)):
                    sin = rope[:, t, 1, lo:lo + D // 2].unsqueeze(1).to_broadcast([P, nh, D // 2])
                    last = nc.vector.tensor_tensor(bv[:, :, lo:lo + D // 2], xv[:, :, hi:hi + D // 2], sin, ALU.mult)
                step(last)
                step(nc.vector.tensor_tensor(av, av, bv, ALU.add))
                for a in range(2):
                    src_q = qk_a[:, t, 0:C].rearrange("p (g a r d) -> p g a r d", a=2, r=4, d=D)[:, :, a]
                    dst_q = stack[0][:, t, 0:H, :].rearrange("p (g r a) s -> p g r a s", a=2, r=4)[:, :, :, a, :]
                    put_stack(step, src_q, lambda at: dst_q[:, :, :, at * D:(at + 1) * D], 2, 1)
                src_k = qk_a[:, t, C:QK0].rearrange("p (h d) -> p h d", d=D)
                put_stack(step, src_k, slots(0, t, H, HKV), 1, 2).then_inc(stack_ready[0], 1)

            def head_squares(u, t, step):
                dve.wait_ge(biased_ready, u * NT + t + 1)
                step(nc.vector.tensor_tensor(qk_a[:, t, :], qk[:, t, :], qk[:, t, :], ALU.mult))
                step(nc.vector.tensor_reduce(ss[:, t, :], qk_a[:, t, :].rearrange("p (h d) -> p h d", d=D),
                                             AX.X, ALU.add))

            def head_norms(step):
                i32 = mybir.dt.int32
                step(nc.vector.tensor_scalar(ss[:], ss[:], 1e-24, None, ALU.max))
                step(nc.vector.tensor_scalar(rs[:].bitcast(i32), ss[:].bitcast(i32), -0.5, float(0x5f3759df),
                                             ALU.mult, ALU.add))
                for _ in range(3):
                    step(nc.vector.scalar_tensor_tensor(nt_a[:], rs[:], -0.5, rs[:], ALU.mult, ALU.mult))
                    step(nc.vector.tensor_tensor(nt_b[:], nt_a[:], ss[:], ALU.mult))
                    step(nc.vector.scalar_tensor_tensor(rs[:], nt_b[:], 1.5, rs[:], ALU.add, ALU.mult))
                step(nc.vector.tensor_tensor(rs[:, :, 0:H], rs[:, :, 0:H],
                                             sm[:].unsqueeze(1).to_broadcast([P, NT, H]), ALU.mult))

            def norm_stack(t, step):
                step(nc.vector.tensor_tensor(
                    qk_b[:, t, :].rearrange("p (h d) -> p h d", d=D), qk[:, t, :].rearrange("p (h d) -> p h d", d=D),
                    rs[:, t, :].unsqueeze(2).to_broadcast([P, 2 * H, D]), ALU.mult))
                src_q = qk_b[:, t, 0:C].rearrange("p (h d) -> p h d", d=D)
                src_k = qk_b[:, t, C:2 * C].rearrange("p (h d) -> p h d", d=D)
                put_stack(step, src_q, slots(1, t, 0, H), 2, 1)
                put_stack(step, src_k, slots(1, t, H, H), 1, 2).then_inc(stack_ready[1], 1)

            def take_fills(u, L):
                for n in FILL_DVE[L]:
                    blk = 2 * FILL_ORDER[L][n]
                    dve.wait_ge(fill_done[L], u * FILLS[L] + n + 1)
                    nc.vector.tensor_copy(qkT[L][:, blk:blk + 2, :],
                                          ps[:, FILL_BANK[L][n], :].rearrange("p (j t) -> p j t", j=2))\
                        .then_inc(fill_dve[L], 1)

            def maxima(i, L, g, uses):
                for n in uses:
                    s = S_USES[L] * g + n
                    dve.wait_ge(s_done[L], i * S_ALL[L] + s + 1)
                    heads, t, nh = score_use(L, g, n)
                    nc.vector.tensor_reduce(negmax[:, heads:heads + nh, t],
                                            ps[:, SB + s % 2, :].rearrange("p (h k) -> p h k", h=nh),
                                            AX.X, ALU.max, negate=True).then_inc(max_done[L], 1)

            def cut_maxima(i, L, g, step):
                dve.wait_ge(max_done[L], i * S_ALL[L] + S_USES[L] * (g + 1))
                nm = negmax[:, GROUP * g:GROUP * (g + 1), :].rearrange("p h t -> p t h")
                step(nc.vector.tensor_copy(m_parts[:, g, :, :, 0].bitcast(f32r), nm))
                nc.vector.tensor_tensor(m_parts[:, g, :, :, 1], nm, m_parts[:, g, :, :, 0],
                                        ALU.subtract).then_inc(m_ready[L], 1)

            def divide(i, L, g, step):
                dve.wait_ge(otr_done[L], i * NG + g + 1)
                ov = ps[:, MB, 0:2 * P].rearrange("p (t h s) -> p t h s", t=NT, h=GROUP)
                step(nc.vector.reciprocal(den[:], ov[:, :, :, D]))
                for t in range(NT):
                    og = o[:, t, g * GROUP * D:(g + 1) * GROUP * D]
                    ogv, ovv = og.rearrange("p (h d) -> p h d", d=D), ov[:, t, :, 0:D]
                    dv = den[:, t, :].unsqueeze(2).to_broadcast([P, GROUP, D])
                    if L == 1:
                        ogv = og.rearrange("p (b a d) -> p a b d", a=2, d=D)
                        ovv = ovv.rearrange("p (a b) d -> p a b d", a=2)
                        dv = den[:, t, :].rearrange("p (a b) -> p a b", a=2).unsqueeze(3).to_broadcast([P, 2, 2, D])
                    last = nc.vector.tensor_tensor(ogv, ovv, dv, ALU.mult)
                last.then_inc(o_ready[L], 1)

            def residual(i, L, step):
                if L == 1:
                    dve.wait_ge(xb_ready[1], i + 1)
                dve.wait_ge(proj_done[L], i + 1)
                new = ps[:, OB, :].rearrange("p (t c) -> p t c", t=NT)
                if L == 1:
                    step(nc.vector.tensor_tensor(
                        scaled[:], new, gamma[:, i, 0, :].unsqueeze(1).to_broadcast([P, NT, C]), ALU.mult))
                    new = scaled[:]
                for t in range(NT):
                    nc.vector.tensor_tensor(xs[:, i, t, :], xs[:, i, t, :], new[:, t, :],
                                            ALU.add).then_inc(x_ready[L], 1)

            def prepare(u, L):
                step, finish = chain(pre_seq[L], u, SEQ_P[L])
                norm_stats(u, L, step)
                norm_apply(u, L)
                for t in range(NT):
                    rope_stack(u, t, step)
                take_fills(u, L)
                finish()

            def finishing(i, L):
                step, finish = chain(fin_seq[L], i, SEQ_F[L])

                def last_residual():
                    residual(i, L, step)
                    finish()
                return lambda: divide(i, L, NG - 1, step), last_residual

            def attention(i, L, before, u, LN):
                step, finish = chain(att_seq[L], i, SEQ_A[L])
                pre, pre_finish = chain(pre_seq[LN], u, SEQ_P[LN])
                uses = S_USES[L]
                if before is not None:
                    last_divide, last_residual = finishing(before[1], before[0])
                    last_divide()
                maxima(i, L, 0, range(uses))
                cut_maxima(i, L, 0, step)
                norm_stats(u, LN, pre)
                maxima(i, L, 1, range(0, 2))
                norm_apply(u, LN)
                maxima(i, L, 1, range(2, uses))
                cut_maxima(i, L, 1, step)
                if before is not None:
                    last_residual()
                maxima(i, L, 2, range(uses))
                cut_maxima(i, L, 2, step)
                if LN == 0:
                    rope_stack(u, 0, pre)
                if LN == 1:
                    head_squares(u, 0, pre)
                maxima(i, L, 3, range(uses))
                cut_maxima(i, L, 3, step)
                divide(i, L, 0, step)
                if LN == 0:
                    rope_stack(u, 1, pre)
                divide(i, L, 1, step)
                if LN == 1:
                    head_squares(u, 1, pre)
                    head_norms(pre)
                    norm_stack(0, pre)
                    norm_stack(1, pre)
                if LN < 2:
                    take_fills(u, LN)
                divide(i, L, 2, step)
                finish()
                pre_finish()

            def mlp(i, last):
                if not last:
                    pre, pre_finish = chain(pre_seq[2], i + 1, SEQ_P[2])
                    norm_stats(i + 1, 2, pre)
                    norm_apply(i + 1, 2)
                    pre_finish()
                dve.wait_ge(xb_ready[2], i + 1)
                for t in range(NT):
                    dve.wait_ge(fc2_done, i * NT + t + 1)
                    nc.vector.tensor_tensor(scaled[:, t, :], ps[:, SB + t, 0:C], gamma[:, i, 1, :], ALU.mult)\
                        .then_inc(scaled_ready[2], 1)
                    dve.wait_ge(scaled_ready[2], i * NT + t + 1)
                    nc.vector.tensor_tensor(xs[:, i, t, :], scaled[:, t, :], xs[:, i, t, :],
                                            ALU.add).then_inc(y_ready, 1)

            dve.wait_ge(x_first, 16)
            prepare(0, 0)
            dve.wait_ge(x_rest, 16)
            attention(0, 0, None, 1, 0)
            with dve.Fori(1, B - 1) as i:
                attention(i, 0, (0, i - 1), i + 1, 0)
            attention(B - 1, 0, (0, B - 2), 0, 1)
            attention(0, 1, (0, B - 1), 1, 1)
            with dve.Fori(1, B - 1) as i:
                attention(i, 1, (1, i - 1), i + 1, 1)
            attention(B - 1, 1, (1, B - 2), 0, 2)
            last_divide, last_residual = finishing(B - 1, 1)
            last_divide()
            last_residual()
            with dve.Fori(0, B - 1) as i:
                mlp(i, False)
            mlp(B - 1, True)

        @block.tensor
        def _(pe):
            mm, tr = nc.tensor.matmul, nc.tensor.transpose
            pe.wait_ge(cond_in, COND_IN)
            pe.wait_ge(silu_ready, 1)
            for a in range(NADA):
                for k in range(NC):
                    if a < ADA0:
                        w, rhs = w_ada_sb[:, k, a * P:(a + 1) * P], condT_sb[:, k, :]
                    else:
                        col = 2 * C + (a - ADA0) * P
                        w, rhs = w_ada1_sb[:, k, col:col + P], siluT[:, k, :]
                    last = mm(ps[:, 0, a * B:(a + 1) * B], w, rhs, start=k == 0, stop=k == NC - 1)
            last.then_inc(setup_mm, 1)
            pe.wait_ge(consts_in, CONSTS_IN)
            for k in range(NC):
                last = mm(ps[:, 1, k * 2 * KVW:(k + 1) * 2 * KVW], wkd_sb[:, k * P:(k + 1) * P], wkuv_sb[:],
                          start=True, stop=True)
            last.then_inc(setup_mm, 1)
            for b in range(B):
                for k in range(NC):
                    last = mm(ps[:, 2 + b, :], silu_b[:, k, b, :], w_ada1_sb[:, k, 0:2 * C],
                              start=k == 0, stop=k == NC - 1)
                last.then_inc(setup_mm, 1)
            pe.wait_ge(rows_counted, 1)
            mm(ps[0:1, 6, 0:1], biased_rows[:], ones[:], start=True, stop=True).then_inc(count_done, 1)
            pe.wait_ge(setup_dve, 7)
            pe.wait_ge(late_in, LATE_IN)
            pe.wait_ge(dve_setup, 13)
            pe.wait_ge(flag_ready, 1)
            biased = nc.tensor.value_load(biased_flag[0:1, 0:1], min_val=0, max_val=1)

            def transposed_norm(u, L):
                for t in range(NT):
                    pe.wait_ge(xn_ready[L], u * NT + t + 1)
                    for c in range(NC):
                        last = tr(ps[:, XB, c * T + t * P:c * T + (t + 1) * P], xn[:, t, c * P:(c + 1) * P], ident[:])
                last.then_inc(xnT_done[L], 1)

            def project_qkv(u, L, n):
                if n == 0:
                    pe.wait_ge(hT_ready[L], u * NC + NC)
                else:
                    pe.wait_ge(raw_ready[L], u * QKV_USES[L] + n)
                w = w0_sb if L == 0 else wqkv_sb
                if L == 0:
                    parts = ((n, 0, 0, W0),)
                elif n < NT:
                    parts = ((n, 0, 0, 2 * C),)
                else:
                    parts = tuple((t, t * C, 2 * C, 3 * C) for t in range(NT))
                for t, col, n0, n1 in parts:
                    for c in range(NC):
                        last = mm(ps[:, XB, col:col + n1 - n0], hT[:, c, t * P:(t + 1) * P], w[:, c, n0:n1],
                                  start=c == 0, stop=c == NC - 1)
                last.then_inc(qkv_done[L], 1)

            def transposed_stacks(u, L, n, before):
                if n == 0:
                    pe.wait_ge(stack_ready[L], u * NT + NT)
                    pe.wait_ge(raw_ready[L], (u + 1) * QKV_USES[L])
                    if before is not None:
                        pe.wait_ge(max_done[before[0]], (before[1] + 1) * S_ALL[before[0]])
                if n == 3 and before is not None:
                    pe.wait_ge(exp_done[before[0]], (before[1] + 1) * H)
                if n in (6, 7):
                    if n == 6:
                        pe.wait_ge(fill_act[L], u * N_ACT[L] + 2)
                    else:
                        pe.wait_ge(fill_dve[L], u * N_DVE[L] + 1)
                for j in range(2):
                    blk = 2 * FILL_ORDER[L][n] + j
                    for t in range(NT):
                        last = tr(ps[:, FILL_BANK[L][n], j * T + t * P:j * T + (t + 1) * P],
                                  stack[L][:, t, 2 * blk:2 * blk + 2, :].rearrange("p h s -> p (h s)"), ident[:])
                last.then_inc(fill_done[L], 1)

            def place(L, h):
                h = head_at(L, h)
                if L == 0:
                    return (h // 8) * 4 + h % 4, H // 2 + h // 8, SLOT * ((h // 4) % 2)
                return h // 2, H // 2 + h // 2, SLOT * (h % 2)

            def scores(i, L, g, n, masked):
                s = S_USES[L] * g + n
                if s >= 2:
                    pe.wait_ge(max_done[L], i * S_ALL[L] + s - 1)
                bank = ps[:, SB + s % 2, :]
                heads, t, nh = score_use(L, g, n)
                keys = P if L == 0 and t == 0 else T
                if L == 0:
                    hide = hide_q[:, 0:P] if t == 0 else hide_q[:, P:3 * P]
                    mm(bank, ident_b[:], hide.unsqueeze(1).to_broadcast([P, nh, keys]), start=True, stop=False)
                elif masked:
                    for j, part in enumerate((bias_hi, bias_lo)):
                        mm(bank, ident_r[:], part[:, 0, t, :].unsqueeze(1).to_broadcast([P, nh, keys]),
                           start=j == 0, stop=False)
                for j in range(nh):
                    qb, kb, half = place(L, heads + j)
                    last = mm(bank[:, j * keys:(j + 1) * keys],
                              qkT[L][half:half + STACK, qb, t * P:(t + 1) * P],
                              qkT[L][half:half + STACK, kb, 0:keys], start=not masked,
                              stop=not masked or j == nh - 1)
                last.then_inc(s_done[L], 1)

            def transposed_maxima(i, L, g):
                pe.wait_ge(m_ready[L], i * NG + g + 1)
                if g >= 3:
                    pe.wait_ge(o_ready[L], i * NG + g - 2)
                for at, t in enumerate((0, 1, 1) if L == 0 else (0, 1)):
                    last = tr(ps[0:2 * GROUP, MB, at * P:(at + 1) * P],
                              m_parts[:, g, t].rearrange("p h a -> p (h a)"), ident[:])
                last.then_inc(mT_done[L], 1)

            def scores_T(i, L, g, j, masked):
                n = GROUP * g + j
                if j == 0:
                    pe.wait_ge(mT_ready[L], i * NG + g + 1)
                if n >= NTB:
                    pe.wait_ge(exp_done[L], i * H + n - NTB + 1)
                qb, kb, half = place(L, n)
                bank = ps[:, TB + n % NTB, :]
                if L == 0:
                    mm(bank[:, 0:3 * P], ident_b[:], hide_k[:], start=True, stop=False)
                    mm(bank[:, 0:3 * P], sel[:, j, :], mT[:, g % 2, :], start=False, stop=False)
                    spans = ((0, 0, 0, T), (1, T, P, T))
                else:
                    if masked:
                        for a, part in enumerate((bias_hi, bias_lo)):
                            mm(bank, ident_r[:], part[:, 1].rearrange("p t q -> p (t q)"), start=a == 0, stop=False)
                    mm(bank, sel[:, j, :], mT[:, g % 2, 0:T].unsqueeze(1).to_broadcast([2 * GROUP, 2, T]),
                       start=not masked, stop=False)
                    spans = ((0, 0, 0, T), (1, T, 0, T))
                for kt, col, q0, q1 in spans:
                    last = mm(bank[:, col:col + q1 - q0], qkT[L][half:half + STACK, kb, kt * P:(kt + 1) * P],
                              qkT[L][half:half + STACK, qb, q0:q1], start=False, stop=kt == 1)
                last.then_inc(st_done[L], 1)

            def outputs(i, L, g):
                if g == 0:
                    pe.wait_ge(v_ready[L], i + 1)
                else:
                    pe.wait_ge(oT_evac[L], i * NG + g)
                pe.wait_ge(exp_done[L], i * H + GROUP * (g + 1))
                for kt in range(2):
                    q0 = P if L == 0 and kt == 1 else 0
                    for j in range(GROUP):
                        vh = g if L == 0 else head_at(L, GROUP * g + j)
                        last = mm(ps[2 * D * j:2 * D * (j + 1), OB, q0:T], vaug[L][:, kt, vh, :],
                                  prob[:, g % 2, j, kt * T:kt * T + T - q0], start=kt == 0, stop=kt == 1)
                last.then_inc(av_done[L], 1)

            def transposed_outputs(i, L, g):
                pe.wait_ge(oT_evac[L], i * NG + g + 1)
                pe.wait_ge(mT_ready[L], i * NG + min(g + 3, NG))
                if g >= 1:
                    pe.wait_ge(o_ready[L], i * NG + g)
                for t in range(NT):
                    last = tr(ps[:, MB, t * P:(t + 1) * P], oT_raw[:, g % 2, t * P:(t + 1) * P], ident[:])
                last.then_inc(otr_done[L], 1)

            def prepare(u, L):
                transposed_norm(u, L)
                for n in range(QKV_USES[L]):
                    project_qkv(u, L, n)
                for n in range(FILLS[L]):
                    transposed_stacks(u, L, n, None)

            def gathered_outputs(i, L):
                pe.wait_ge(o_ready[L], i * NG + NG)
                for c in range(NC):
                    for t in range(NT):
                        last = tr(ps[:, MB, c * T + t * P:c * T + (t + 1) * P], o[:, t, c * P:(c + 1) * P], ident[:])
                last.then_inc(oc_done[L], 1)

            def project_outputs(i, L):
                pe.wait_ge(oc_ready[L], i + 1)
                w = wo_sb if L == 0 else wproj_sb
                for t in range(NT):
                    for c in range(NC):
                        last = mm(ps[:, OB, t * C:(t + 1) * C], oT[:, c, t * P:(t + 1) * P], w[:, c, :],
                                  start=c == 0, stop=c == NC - 1)
                last.then_inc(proj_done[L], 1)

            def attention(i, L, before, u, LN, masked=True):
                uses = S_USES[L]
                if before is not None:
                    transposed_outputs(before[1], before[0], NG - 1)
                pe.wait_ge(fill_act[L], (i + 1) * N_ACT[L])
                pe.wait_ge(fill_dve[L], (i + 1) * N_DVE[L])
                for n in range(uses):
                    if n == uses - 1 and before is not None:
                        gathered_outputs(before[1], before[0])
                    scores(i, L, 0, n, masked)
                for g in range(NG):
                    if g == 0 and before is not None:
                        pe.wait_ge(oc_ready[before[0]], before[1] + 1)
                    transposed_maxima(i, L, g)
                    if g == 0 and before is not None:
                        project_outputs(before[1], before[0])
                    if g >= 1 and LN < 2 and g <= QKV_USES[LN]:
                        project_qkv(u, LN, g - 1)
                    if g >= 2:
                        transposed_outputs(i, L, g - 2)
                    for j in range(GROUP):
                        if g + 1 < NG and j < uses:
                            scores(i, L, g + 1, j, masked)
                        scores_T(i, L, g, j, masked)
                    if g == 0:
                        transposed_norm(u, LN)
                    else:
                        if g == 1 and before is not None:
                            pe.wait_ge(x_ready[before[0]], (before[1] + 1) * NT)
                        outputs(i, L, g - 1)
                fills = FILLS[LN] if LN < 2 else 0
                for n in range(0, min(fills, 3)):
                    transposed_stacks(u, LN, n, (L, i))
                outputs(i, L, NG - 1)
                for n in range(3, fills):
                    transposed_stacks(u, LN, n, (L, i))
                transposed_outputs(i, L, NG - 2)

            def mlp(i, last_one):
                pe.wait_ge(hT_ready[2], i * NC + NC)
                for f in range(NF):
                    if f >= len(GB):
                        pe.wait_ge(gelu_done, i * NF + f - len(GB) + 1)
                    for c in range(NC):
                        last = mm(ps[:, GB[f % len(GB)], 0:T], wfc1_sb[:, c, f * P:(f + 1) * P], hT[:, c, :],
                                  start=c == 0, stop=c == NC - 1)
                    last.then_inc(fc1_done, 1)
                if not last_one:
                    transposed_norm(i + 1, 2)
                else:
                    pe.wait_ge(scaled_ready[2], i * NT)
                for t in range(NT):
                    for f in range(NF):
                        if t == 0:
                            pe.wait_ge(gelu_done, i * NF + f + 1)
                        last = mm(ps[:, SB + t, 0:C], gT[:, f, t * P:(t + 1) * P], wfc2_sb[:, f, :],
                                  start=f == 0, stop=f == NF - 1)
                    last.then_inc(fc2_done, 1)

            prepare(0, 0)
            attention(0, 0, None, 1, 0)
            with pe.Fori(1, B - 1) as i:
                attention(i, 0, (0, i - 1), i + 1, 0)
            attention(B - 1, 0, (0, B - 2), 0, 1)

            def layer1(masked):
                attention(0, 1, (0, B - 1), 1, 1, masked)
                with pe.Fori(1, B - 1) as i:
                    attention(i, 1, (1, i - 1), i + 1, 1, masked)
                attention(B - 1, 1, (1, B - 2), 0, 2, masked)

            with pe.If(biased):
                layer1(True)
            with pe.Else():
                layer1(False)
            transposed_outputs(B - 1, 1, NG - 1)
            gathered_outputs(B - 1, 1)
            project_outputs(B - 1, 1)
            with pe.Fori(0, B - 1) as i:
                mlp(i, False)
            mlp(B - 1, True)


def score_use(L, g, n):
    if L == 0:
        return (GROUP * g, 0, GROUP) if n == 0 else (GROUP * g + 2 * (n - 1), 1, 2)
    return GROUP * g + 2 * (n // 2), n % 2, 2


def head_at(L, n):
    return n if L == 0 else n // GROUP * GROUP + (0, 2, 1, 3)[n % GROUP]


def kernel(x, cond_2048, mask_1x1xSxS_ff0, L0_cond_W_ada, L0_cond_b_ada, L0_cond_Wq, L0_cond_Wkd, L0_cond_Wku,
           L0_cond_Wvu, L0_cond_Wo, L1_cond_Wqkv, L1_cond_q_bias, L1_cond_v_bias, L1_cond_scale_mul_log,
           L1_cond_Wproj, L1_cond_bproj, L1_cond_Wada, L1_cond_bada, L1_cond_Wfc1, L1_cond_bfc1, L1_cond_Wfc2,
           L1_cond_bfc2):
    import numpy as np
    import concourse.bacc as bacc
    from concourse.bass_utils import run_bass_kernel_spmd

    def arr(a):
        return np.ascontiguousarray(np.asarray(a))

    pos = np.arange(T)
    freqs = (1.0 / np.float32(10000.0) ** (np.arange(0, D, 2, dtype=np.float32) / D)).astype(np.float32)
    angle = pos.astype(np.float32)[:, None] * freqs[None, :]
    rope = np.zeros((T, 2, D), np.float32)
    rope[:, 0, :] = np.concatenate([np.cos(angle), np.cos(angle)], -1)
    rope[:, 1, :] = np.concatenate([-np.sin(angle), np.sin(angle)], -1)
    blk = pos // 128
    hidden = ((np.abs(pos[None, :] - pos[:, None]) > 32) & ~(pos % 64 == 0)[None, :]) | (blk[None, :] > blk[:, None])
    hide = np.where(hidden, np.float32(NEG), np.float32(0.0)).astype(np.float32)
    hide_q = np.concatenate([hide[0:P, 0:P], hide[P:T, :]], 1)
    hide_k = np.concatenate([hide.T[0:P, :], hide.T[P:T, P:T]], 1)
    sel = np.zeros((2 * GROUP, GROUP, P), np.float32)
    for j in range(GROUP):
        sel[2 * j:2 * j + 2, j, :] = 1.0

    bada, wada = arr(L1_cond_bada), arr(L1_cond_Wada)
    mask = arr(mask_1x1xSxS_ff0).reshape(T, T)
    arrays = {
        "x": arr(x),
        "condT": arr(arr(cond_2048).T),
        "w_adaT": arr(arr(L0_cond_W_ada).T),
        "w_ada1T": arr(wada.T),
        "b_adaT": arr(np.concatenate([arr(L0_cond_b_ada), bada[2 * C:]]).reshape(NADA, P).T),
        "b_gamma": bada[0:2 * C],
        "wqT": arr(arr(L0_cond_Wq).T),
        "wkd": arr(L0_cond_Wkd),
        "wkuvT": arr(np.concatenate([arr(L0_cond_Wku), arr(L0_cond_Wvu)], 0).T),
        "woT": arr(arr(L0_cond_Wo).T),
        "wqkvT": arr(arr(L1_cond_Wqkv).T),
        "q_bias": arr(L1_cond_q_bias),
        "v_bias": arr(L1_cond_v_bias),
        "scale_log": arr(L1_cond_scale_mul_log).reshape(H),
        "wprojT": arr(arr(L1_cond_Wproj).T),
        "bproj": arr(L1_cond_bproj),
        "wfc1T": arr(arr(L1_cond_Wfc1).T),
        "bfc1T": arr(arr(L1_cond_bfc1).reshape(NF, P).T),
        "wfc2T": arr(arr(L1_cond_Wfc2).T),
        "bfc2": arr(L1_cond_bfc2),
        "bias_q": mask,
        "bias_k": arr(mask.T),
        "ident_d": np.eye(P, dtype=np.float32),
        "rope_d": rope,
        "hide_q_d": arr(hide_q),
        "hide_k_d": arr(hide_k),
        "sel_d": sel,
    }
    nc = bacc.Bacc("TRN2", target_bir_lowering=False, num_devices=1)
    aps = {n: nc.dram_tensor("in_" + n, a.shape, mybir.dt.from_np(a.dtype), kind="ExternalInput").ap()
           for n, a in arrays.items()}
    out = nc.dram_tensor("out_0", (B, T, C), mybir.dt.float32, kind="ExternalOutput").ap()
    build(nc, out=out, **aps)
    r = run_bass_kernel_spmd(nc, [{"in_" + n: a for n, a in arrays.items()}], core_ids=[0])
    return r.results[0]["out_0"]
```

```python
import concourse.bass as bass
from concourse import mybir
from contextlib import ExitStack

B, T, C = 4, 256, 256
P = 128
NT, NC = T // P, C // P
H, D, HKV = 16, 16, 4
GROUP = 4
NG = H // GROUP
HID = 4 * C
NF = HID // P
SLOT = 64
STACK = 3 * D
KVW = HKV * D
QK0 = C + KVW
W0 = C + 2 * KVW
NEG = -1e30
LOWEST = -3e38
LN0_EPS, LN1_EPS = 1e-5, 1e-6
ADA0, ADA1 = 4, 8
NADA = ADA0 + ADA1

SB = 0
TB, NTB = 2, 3
OB = 5
MB = 6
PB = TB + 1
XB = 7

S_USES = (3, 4)
S_ALL = (S_USES[0] * NG, S_USES[1] * NG)
FILL_BLOCKS = (((0, 1), (2, 3), (8,), (4, 5), (6, 7), (12,)),
               ((0, 1), (8, 9), (2, 3), (10, 11), (4, 5), (12, 13), (6, 7), (14, 15)))
FILLS = (len(FILL_BLOCKS[0]), len(FILL_BLOCKS[1]))
FIRST_FILLS, FILLS_AHEAD = (3, 2), 5
FILL_BANK = (XB, SB + 1, XB, XB, XB, OB, XB, OB)
FILL_BANK_0 = (XB, SB + 1, OB, MB, XB)
LAST_IN_PB = max(n for n in range(H) if TB + n % NTB == PB)
QKV_USES = (2, 3)
GB = (2, 3, 4)
SEQ_P, SEQ_S = (11, 21, 1), 2


def build(nc, x, condT, w_adaT, w_ada1T, b_adaT, b_ada1, wqT, wkd, wkuvT, woT, wqkvT, q_bias, v_bias,
          scale_log, wprojT, bproj, wfc1T, bfc1T, wfc2T, bfc2, bias_q, bias_k, ident_d, rope_d, hide_q_d,
          hide_k_d, sel_d, out):
    f32, f32r, bf16 = mybir.dt.float32, mybir.dt.float32r, mybir.dt.bfloat16
    ALU, ACT, AX = mybir.AluOpType, mybir.ActivationFunctionType, mybir.AxisListType

    ctx = ExitStack()
    with ctx:
        def sb(name, shape, dt=f32):
            return ctx.enter_context(nc.sbuf_tensor(name, shape, dt))

        def sem(name):
            return ctx.enter_context(nc.semaphore(name))

        condT_sb = sb("condT_sb", [P, NC, B])
        w_ada_sb = sb("w_ada_sb", [P, NC, 2 * C])
        w_ada1_sb = sb("w_ada1_sb", [P, NC, 6 * C])
        b_ada_sb = sb("b_ada_sb", [P, ADA0])
        b_ada1_sb = sb("b_ada1_sb", [B, 6 * C])
        w0_sb = sb("w0_sb", [P, NC, W0])
        wkd_sb = sb("wkd_sb", [64, C])
        wkuv_sb = sb("wkuv_sb", [64, 2 * KVW])
        wo_sb = sb("wo_sb", [P, NC, C])
        wqkv_sb = sb("wqkv_sb", [P, NC, 3 * C])
        wproj_sb = sb("wproj_sb", [P, NC, C])
        wfc1_sb = w_ada1_sb[:].rearrange("p k n -> p (k n)")[:, 0:NC * HID].rearrange("p (k n) -> p k n", k=NC)
        wfc2_sb = w_ada1_sb[:].rearrange("p k n -> p (k n)")[:, 0:NF * C].rearrange("p (k n) -> p k n", k=NF)
        bfc1_sb = sb("bfc1_sb", [P, NF])
        qv_bias_sb = sb("qv_bias_sb", [P, 2, C])
        out_bias_sb = sb("out_bias_sb", [P, 2, C])
        scale_sb = sb("scale_sb", [P, H])
        ident = sb("ident", [P, P])
        ident_b = sb("ident_b", [P, P], bf16)
        ident_r = sb("ident_r", [P, P], f32r)
        rope = sb("rope", [P, NT, 2, D])
        hide_f = sb("hide_f", [P, 2, 384])
        hide_q = sb("hide_q", [P, 384], bf16)
        hide_k = sb("hide_k", [P, 384], bf16)
        sel_f = sb("sel_f", [2 * GROUP, GROUP, P])
        sel = sb("sel", [2 * GROUP, GROUP, P], f32r)
        bias_f = sb("bias_f", [P, 2, NT, T])
        bias_hi = sb("bias_hi", [P, 2, NT, T], f32r)
        bias_lo = sb("bias_lo", [P, 2, NT, T], f32r)
        biased_f = w_ada_sb[:].rearrange("p k n -> p (k n)").rearrange("p (a t k) -> p a t k", a=2, t=NT)
        biased_rows = sb("biased_rows", [P, 1])
        ones = sb("ones", [P, 1])
        biased_flag = sb("biased_flag", [1, 1], mybir.dt.int32)
        silu_e = sb("silu_e", [P, NC, B])
        silu_d = sb("silu_d", [P, NC, B])
        silu_r = sb("silu_r", [P, NC, B])
        siluT = sb("siluT", [P, NC, B])
        adaT = sb("adaT", [P, NADA, B])
        gamma = sb("gamma", [P, B, 2, C])
        gamma_dram = nc.dram_tensor("gamma_dram", [B, 2 * C], f32, kind="Internal").ap()
        sm_l = sb("sm_l", [P, H])
        sm = sb("sm", [P, H])
        xs = sb("xs", [P, B, NT, C])
        bg = sb("bg", [P, B, 2, C])
        ada1_rows = bg[0:B].rearrange("p b a c -> p (b a c)")[:, 0:6 * C]
        ada_now = sb("ada_now", [P, NADA])
        stats = sb("stats", [P, NT, 6])
        mv = sb("mv", [P, NT, 2])
        mean = sb("mean", [P, B, NT])
        wait_here = sb("wait_here", [P, 1])
        var_eps = sb("var_eps", [P, B, NT])
        rstd = sb("rstd", [P, B, NT])
        minus_half = sb("minus_half", [P, NT])
        xn = sb("xn", [P, NT, C])
        hT = sb("hT", [P, NC, T])
        qk = sb("qk", [P, NT, 2 * C])
        qk_a = sb("qk_a", [P, NT, 2 * C])
        qk_b = sb("qk_b", [P, NT, 2 * C])
        ss = sb("ss", [P, NT, 2 * H])
        nt_a = sb("nt_a", [P, NT, 2 * H])
        nt_b = sb("nt_b", [P, NT, 2 * H])
        rs = sb("rs", [P, NT, 2 * H])
        stack = sb("stack", [P, NT, 2 * H, SLOT])
        qkT = sb("qkT", [P, H, T], f32r)
        vaug = [sb("vaug0", [P, NT, HKV, 2 * D]), sb("vaug1", [P, NT, H, 2 * D])]
        vraw = sb("vraw", [P, NT, C])
        negmax = sb("negmax", [P, H, NT])
        m_parts = sb("m_parts", [P, NG, NT, GROUP, 2])
        mT = sb("mT", [2 * GROUP, 2, 3 * P], f32r)
        prob = sb("prob", [P, 2, GROUP, 2 * T])
        oT_raw = sb("oT_raw", [P, 2, T])
        den = sb("den", [P, NT, GROUP])
        o = sb("o", [P, NT, C])
        oT = sb("oT", [P, NC, T])
        scaled = sb("scaled", [P, NT, C])
        w1_hi, w1_lo = sb("w1_hi", [P, NC, HID], f32r), sb("w1_lo", [P, NC, HID], f32r)
        w2_hi, w2_lo = sb("w2_hi", [P, NF, C], f32r), sb("w2_lo", [P, NF, C], f32r)
        h_hi, h_lo = bias_hi[:, 0], bias_lo[:, 0]
        g_hi, g_lo = qkT[:, 0:NF, :], qkT[:, NF:2 * NF, :]
        gT = prob[:].rearrange("p a h q -> p (a h q)")[:, 0:NF * T].rearrange("p (f q) -> p f q", f=NF)
        ps = ctx.enter_context(nc.psum_tensor("ps", [P, 8, 512], f32))

        cond_in, ada0_in, ident_in, w0_in = sem("cond_in"), sem("ada0_in"), sem("ident_in"), sem("w0_in")
        rope_in, ada1_in, hide_in, scale_in = sem("rope_in"), sem("ada1_in"), sem("hide_in"), sem("scale_in")
        mask_in, late_in, wfc_in = sem("mask_in"), sem("late_in"), sem("wfc_in")
        silu_exp, silu_ready, sm_ready, sm_min = sem("silu_exp"), sem("silu_ready"), sem("sm_ready"), sem("sm_min")
        dve_setup, setup_mm, pads_set = sem("dve_setup"), sem("setup_mm"), sem("pads_set")
        w0_ready, consts_ready, ada1_ready = sem("w0_ready"), sem("consts_ready"), sem("ada1_ready")
        rows_ready, gamma_stored, gamma_in, mask_ready = sem("rows_ready"), sem("gamma_stored"), sem("gamma_in"), sem("mask_ready")
        rows_counted, count_done, flag_ready = sem("rows_counted"), sem("count_done"), sem("flag_ready")
        x_first, x_rest = sem("x_first"), sem("x_rest")

        def per_layer(name, n=2):
            return [sem(f"{name}{L}") for L in range(n)]
        stats_seq, pre_seq = per_layer("stats_seq", 3), per_layer("pre_seq", 3)
        xn_ready, xnT_done = per_layer("xn_ready", 3), per_layer("xnT_done", 3)
        var_ready, rstd_ready, hT_ready = per_layer("var_ready", 3), per_layer("rstd_ready", 3), per_layer("hT_ready", 3)
        qkv_done, raw_ready, v_ready = per_layer("qkv_done"), per_layer("raw_ready"), per_layer("v_ready")
        biased_ready, squares_ready = sem("biased_ready"), sem("squares_ready")
        lo_ready = sem("lo_ready")
        stack_ready = per_layer("stack_ready")
        fill_done, fill_ready = per_layer("fill_done"), per_layer("fill_ready")
        max_cut, den_ready = per_layer("max_cut"), per_layer("den_ready")
        s_done, max_done, m_ready = per_layer("s_done"), per_layer("max_done"), per_layer("m_ready")
        mT_done, mT_ready = per_layer("mT_done"), per_layer("mT_ready")
        st_done, exp_done, av_done = per_layer("st_done"), per_layer("exp_done"), per_layer("av_done")
        oT_evac, otr_done, o_ready = per_layer("oT_evac"), per_layer("otr_done"), per_layer("o_ready")
        oc_done, oc_ready = per_layer("oc_done"), per_layer("oc_ready")
        proj_done, x_ready = per_layer("proj_done"), per_layer("x_ready")
        bg_ready, xb_ready, scaled_ready = sem("bg_ready"), per_layer("xb_ready", 3), per_layer("scaled_ready", 3)
        w_hi_ready, w_lo_ready, h_hi_ready, h_parts = sem("w_hi_ready"), sem("w_lo_ready"), sem("h_hi_ready"), sem("h_parts")
        g_hi_ready, g_parts = sem("g_hi_ready"), sem("g_parts")
        fc1_done, gelu_done, fc2_done = sem("fc1_done"), sem("gelu_done"), sem("fc2_done")
        y_ready, y_stored = sem("y_ready"), sem("y_stored")

        ADA0_IN, W0_IN, ADA1_IN, HIDE_IN, MASK_IN, LATE_IN = 2 * 16, 3 * 16, 2 * 16, 3 * 16, 2 * 16, 9 * 16
        block = ctx.enter_context(nc.Block())

        x_v = x.rearrange("b (t p) c -> b p t c", p=P)
        out_v = out.rearrange("b (t p) c -> b p t c", p=P)

        def wide(w):
            return w.rearrange("(k p) n -> p k n", p=P)

        def rows(v):
            return v.partition_broadcast(P)

        @block.sync
        def _(sp):
            sp.dma_start(xs[:, 0], x_v[0]).then_inc(x_first, 16)
            sp.dma_start(wkd_sb[:], wkd).then_inc(w0_in, 16)
            sp.dma_start(wkuv_sb[:], wkuvT).then_inc(w0_in, 16)
            sp.dma_start(w_ada_sb[:], wide(w_adaT)).then_inc(ada0_in, 16)
            sp.dma_start(w0_sb[:, :, 0:C], wide(wqT)).then_inc(w0_in, 16)
            sp.dma_start(rope[:], rope_d.rearrange("(t p) a d -> p t a d", p=P)).then_inc(rope_in, 16)
            sp.dma_start(w_ada1_sb[:], wide(w_ada1T)).then_inc(ada1_in, 16)
            sp.dma_start(b_ada1_sb[:], b_ada1.partition_broadcast(B)).then_inc(ada1_in, 16)
            sp.dma_start(hide_f[:, 0, :], hide_q_d).then_inc(hide_in, 16)
            sp.dma_start(hide_f[:, 1, :], hide_k_d).then_inc(hide_in, 16)
            sp.dma_start(sel_f[:], sel_d).then_inc(hide_in, 16)
            sp.dma_start(bias_f[:, 0], bias_q.rearrange("(t p) k -> p t k", p=P)).then_inc(mask_in, 16)
            sp.dma_start(bias_f[:, 1], bias_k.rearrange("(t p) k -> p t k", p=P)).then_inc(mask_in, 16)
            sp.dma_start(xs[:, 1:B].rearrange("p b t c -> p (b t) c"),
                         x[1:B].rearrange("b (t p) c -> p (b t) c", p=P)).then_inc(x_rest, 16)
            sp.dma_start(wo_sb[:], wide(woT)).then_inc(late_in, 16)
            sp.dma_start(wqkv_sb[:, 0, :], wqkvT[0:P, :]).then_inc(late_in, 16)
            sp.dma_start(wqkv_sb[:, 1, :], wqkvT[P:C, :]).then_inc(late_in, 16)
            sp.wait_ge(rows_ready, 1)
            sp.dma_start(gamma_dram, ada1_rows[:, 0:2 * C]).then_inc(gamma_stored, 16)
            sp.wait_ge(gamma_stored, 16)
            sp.dma_start(gamma[:].rearrange("p b a c -> p (b a c)"),
                         rows(gamma_dram.rearrange("b c -> (b c)"))).then_inc(gamma_in, 16)
            sp.dma_start(qv_bias_sb[:, 0], rows(q_bias)).then_inc(late_in, 16)
            sp.dma_start(qv_bias_sb[:, 1], rows(v_bias)).then_inc(late_in, 16)
            sp.dma_start(out_bias_sb[:, 0], rows(bproj)).then_inc(late_in, 16)
            sp.dma_start(out_bias_sb[:, 1], rows(bfc2)).then_inc(late_in, 16)
            sp.dma_start(wproj_sb[:], wide(wprojT)).then_inc(late_in, 16)
            sp.dma_start(bfc1_sb[:], bfc1T).then_inc(late_in, 16)
            sp.wait_ge(setup_mm, 3)
            sp.dma_start(wfc1_sb, wide(wfc1T)).then_inc(wfc_in, 16)
            sp.wait_ge(w_lo_ready, 1)
            sp.dma_start(wfc2_sb, wide(wfc2T)).then_inc(wfc_in, 16)
            with sp.Fori(0, B) as i:
                sp.wait_ge(y_ready, i * NT + NT)
                sp.dma_start(out_v[i], xs[:, i]).then_inc(y_stored, 16)
            sp.wait_ge(y_stored, B * 16)

        @block.gpsimd
        def _(pool):
            pool.memset(stack[:, :, :, STACK:SLOT], 0.0).then_inc(pads_set, 1)
            for v in vaug:
                pool.memset(v[:, :, :, D:2 * D], 1.0).then_inc(pads_set, 1)
            pool.memset(minus_half[:], -0.5).then_inc(pads_set, 1)
            pool.wait_ge(pads_set, 4)

            def make_rstd(u, L):
                pool.wait_ge(var_ready[L], u + 1)
                pool.tensor_tensor(rstd[:, u], var_eps[:, u], minus_half[:], ALU.pow).then_inc(rstd_ready[L], 1)

            def prepare(u, L, before=None):
                if L > 0:
                    pool.wait_ge(xn_ready[L], u * NT + NT)
                    pool.tensor_tensor(xs[:, u], xs[:, u], bg[:, u, L - 1].unsqueeze(1).to_broadcast([P, NT, C]),
                                       ALU.add).then_inc(xb_ready[L], 1)
                if L == 1:
                    for t in range(NT):
                        pool.wait_ge(raw_ready[1], u * QKV_USES[1] + t + 1)
                        pool.tensor_tensor(qk[:, t, 0:C], qk[:, t, 0:C], qv_bias_sb[:, 0], ALU.add)\
                            .then_inc(biased_ready, 1)
                        pool.wait_ge(biased_ready, u * NT + t + 1)
                        pool.tensor_tensor(qk_a[:, t, :], qk[:, t, :], qk[:, t, :], ALU.mult).then_inc(squares_ready, 1)
                if L < 2:
                    if L == 1:
                        for t in range(NT):
                            for part in range(2):
                                pool.wait_ge(stack_ready[1], u * 2 * NT + 2 * t + part + 1)
                                heads = stack[:, t, part * H:(part + 1) * H, :]
                                lo = heads[:, :, D:2 * D] if part == 0 else heads[:, :, 2 * D:3 * D]
                                pool.tensor_tensor(lo, qk_b[:, t, part * C:(part + 1) * C].rearrange("p (h d) -> p h d", d=D),
                                                   heads[:, :, 0:D], ALU.subtract).then_inc(lo_ready, 1)
                    pool.wait_ge(raw_ready[L], (u + 1) * QKV_USES[L])
                    if before is not None:
                        pool.wait_ge(av_done[before[0]], (before[1] + 1) * NG)
                    if L == 0:
                        v = vraw[:, :, 0:KVW].rearrange("p t (h d) -> p t h d", d=D)
                        pool.tensor_tensor(vaug[0][:, :, :, 0:D], v, vaug[0][:, :, :, D:2 * D], ALU.mult).then_inc(v_ready[0], 1)
                    else:
                        pool.tensor_tensor(vaug[1][:, :, :, 0:D], vraw[:].rearrange("p t (h d) -> p t h d", d=D),
                                           qv_bias_sb[:, 1].rearrange("p (h d) -> p h d", d=D).unsqueeze(1)
                                           .to_broadcast([P, NT, H, D]), ALU.add).then_inc(v_ready[1], 1)

            make_rstd(0, 0)
            prepare(0, 0)
            for b in range(1, B):
                make_rstd(b, 0)
            pool.wait_ge(late_in, LATE_IN)
            pool.wait_ge(gamma_in, 16)
            pool.wait_ge(ada1_ready, 1)
            for b in range(B):
                pool.tensor_tensor(bg[:, b], out_bias_sb[:], gamma[:, b], ALU.mult).then_inc(bg_ready, 1)
            prepare(1, 0, (0, 0))
            for n, (w, hi, lo) in enumerate(((wfc1_sb, w1_hi, w1_lo), (wfc2_sb, w2_hi, w2_lo))):
                pool.wait_ge(wfc_in, 16 * (n + 1))
                pool.tensor_copy(hi[:], w).then_inc(w_hi_ready, 1)
                pool.wait_ge(w_hi_ready, n + 1)
                pool.tensor_tensor(lo[:], w, hi[:].bitcast(f32), ALU.subtract).then_inc(w_lo_ready, 1)
            with pool.Fori(1, B - 1) as i:
                prepare(i + 1, 0, (0, i))
                make_rstd(i - 1, 1)
            pool.wait_ge(bg_ready, B)
            prepare(0, 1, (0, B - 1))
            make_rstd(B - 2, 1)
            prepare(1, 1, (1, 0))
            make_rstd(B - 1, 1)
            with pool.Fori(1, B - 1) as i:
                prepare(i + 1, 1, (1, i))
                make_rstd(i - 1, 2)
            prepare(0, 2)
            make_rstd(B - 2, 2)
            prepare(1, 2)
            make_rstd(B - 1, 2)
            with pool.Fori(1, B - 1) as i:
                prepare(i + 1, 2)

        @block.scalar
        def _(act):
            act.dma_start(condT_sb[:], condT.rearrange("(k p) b -> p k b", p=P)).then_inc(cond_in, 16)
            act.dma_start(b_ada_sb[:], b_adaT).then_inc(ada0_in, 16)
            act.dma_start(ident[:], ident_d).then_inc(ident_in, 16)
            act.dma_start(scale_sb[:], rows(scale_log)).then_inc(scale_in, 16)
            act.wait_ge(cond_in, 16)
            nc.scalar.activation(silu_e[:], condT_sb[:], ACT.Exp, scale=-1.0).then_inc(silu_exp, 1)

            def modulate(u, L):
                act.wait_ge(xnT_done[L], u + 1)
                at_scale = (0, ADA0, ADA0 + 2)[L]
                at_shift = (2, ADA0 + 4, ADA0 + 6)[L]
                for c in range(NC):
                    nc.scalar.activation(hT[:, c, :], ps[:, XB, c * T:(c + 1) * T], ACT.Identity,
                                         bias=ada_now[:, at_shift + c:at_shift + c + 1],
                                         scale=ada_now[:, at_scale + c:at_scale + c + 1]).then_inc(hT_ready[L], 1)

            def take_qkv(u, L, n):
                if n == QKV_USES[L] - 1 or L == 0:
                    if not isinstance(u, int) or u > 0:
                        act.wait_ge(v_ready[L], u)
                    elif L == 1:
                        act.wait_ge(v_ready[0], B)
                act.wait_ge(qkv_done[L], u * QKV_USES[L] + n + 1)
                if L == 0:
                    nc.scalar.activation(vraw[:, n, 0:KVW], ps[:, XB, QK0:W0], ACT.Copy)
                    ins = nc.scalar.activation(qk[:, n, 0:QK0], ps[:, XB, 0:QK0], ACT.Copy)
                elif n < NT:
                    ins = nc.scalar.activation(qk[:, n, :], ps[:, XB, :], ACT.Copy)
                else:
                    ins = nc.scalar.activation(vraw[:].rearrange("p t c -> p (t c)"), ps[:, XB, :], ACT.Copy)
                ins.then_inc(raw_ready[L], 1)

            def take_fill(u, L, n, banks=FILL_BANK):
                blocks = FILL_BLOCKS[L][n]
                act.wait_ge(fill_done[L], u * FILLS[L] + n + 1)
                nc.scalar.activation(qkT[:, blocks[0]:blocks[0] + len(blocks), :].rearrange("p j t -> p (j t)"),
                                     ps[:, banks[n], 0:len(blocks) * T], ACT.Copy).then_inc(fill_ready[L], 1)

            def prepare(u, L):
                modulate(u, L)
                for n in range(QKV_USES[L]):
                    take_qkv(u, L, n)
                for n in range(FILLS_AHEAD):
                    take_fill(u, L, n, FILL_BANK_0)

            def take_projected(i, L):
                act.wait_ge(oc_done[L], i + 1)
                nc.scalar.activation(oT[:].rearrange("p c t -> p (c t)"), ps[:, MB, :],
                                     ACT.Copy).then_inc(oc_ready[L], 1)

            def take_outputs(i, L, g):
                act.wait_ge(av_done[L], i * NG + g + 1)
                nc.scalar.activation(oT_raw[:, g % 2, :], ps[:, OB, 0:T], ACT.Copy).then_inc(oT_evac[L], 1)

            def attention(i, L, before, u, LN):
                cols = 3 * P if L == 0 else 2 * T
                width = 3 * P if L == 0 else T
                for g in range(NG):
                    act.wait_ge(mT_done[L], i * NG + g + 1)
                    nc.scalar.activation(mT[:, g % 2, 0:width], ps[0:2 * GROUP, MB, 0:width],
                                         ACT.Copy).then_inc(mT_ready[L], 1)
                    if g == 1 and LN < 2:
                        take_qkv(u, LN, 1)
                    if g == 3 and LN == 1:
                        take_qkv(u, LN, 2)
                    for j in range(GROUP):
                        n = GROUP * g + j
                        act.wait_ge(st_done[L], i * H + n + 1)
                        nc.scalar.activation(prob[:, g % 2, j, 0:cols], ps[:, TB + n % NTB, 0:cols], ACT.Exp,
                                             scale=D ** -0.5 if L == 0 else 1.0).then_inc(exp_done[L], 1)
                        if (g, j) == (0, 0):
                            take_fill(i, L, 5)
                        if (g, j) == (0, 1):
                            modulate(u, LN)
                        if L == 1 and (g, j) in ((1, 1), (1, 2)):
                            take_fill(i, L, 5 + j)
                        if LN == 0 and g == 3 and j >= 1:
                            take_fill(u, LN, j - 1)
                    if g == 0 and before is not None:
                        take_projected(before[1], before[0])
                    if g == 0 and LN < 2:
                        take_qkv(u, LN, 0)
                    if g in (1, 2):
                        take_outputs(i, L, g - 1)
                if LN < 2:
                    for n in range(3 * (1 - LN), FIRST_FILLS[LN]):
                        take_fill(u, LN, n)
                take_outputs(i, L, NG - 2)
                if LN < 2:
                    take_fill(u, LN, FIRST_FILLS[LN])
                    take_fill(u, LN, FIRST_FILLS[LN] + 1)
                take_outputs(i, L, NG - 1)
                if LN < 2:
                    for n in range(FIRST_FILLS[LN] + 2, FILLS_AHEAD):
                        take_fill(u, LN, n)

            def gelus(i, hidden):
                for f in hidden:
                    act.wait_ge(fc1_done, i * NF + f + 1)
                    nc.scalar.activation(gT[:, f, :], ps[:, GB[f % len(GB)], 0:T], ACT.Gelu_apprx_tanh,
                                         bias=bfc1_sb[:, f:f + 1]).then_inc(gelu_done, 1)

            prepare(0, 0)
            act.wait_ge(sm_min, 1)
            nc.scalar.activation(sm[:], sm_l[:], ACT.Exp).then_inc(sm_ready, 1)
            attention(0, 0, None, 1, 0)
            with act.Fori(1, B - 1) as i:
                attention(i, 0, (0, i - 1), i + 1, 0)
            attention(B - 1, 0, (0, B - 2), 0, 1)
            attention(0, 1, (0, B - 1), 1, 1)
            with act.Fori(1, B - 1) as i:
                attention(i, 1, (1, i - 1), i + 1, 1)
            attention(B - 1, 1, (1, B - 2), 0, 2)
            act.wait_ge(late_in, LATE_IN)
            gelus(0, range(0, 4))
            take_projected(B - 1, 1)
            gelus(0, range(4, NF))
            modulate(1, 2)
            with act.Fori(1, B - 1) as i:
                gelus(i, range(NF))
                modulate(i + 1, 2)
            gelus(B - 1, range(NF))

        @block.vector
        def _(dve):
            def chain(sem, u, per):
                n = [0]

                def step(ins):
                    n[0] += 1
                    ins.then_inc(sem, 1)
                    dve.wait_ge(sem, u * per + n[0])

                def finish():
                    assert n[0] == per, (sem, n[0], per)
                return step, finish

            setup = [0]

            def done(ins):
                setup[0] += 1
                ins.then_inc(dve_setup, 1)
                dve.wait_ge(dve_setup, setup[0])

            nc.vector.memset(ones[:], 1.0)
            done(nc.vector.memset(adaT[:], 0.0))
            dve.wait_ge(silu_exp, 1)
            done(nc.vector.tensor_scalar(silu_d[:], silu_e[:], 1.0, None, ALU.add))
            done(nc.vector.reciprocal(silu_r[:], silu_d[:]))
            nc.vector.tensor_tensor(siluT[:], condT_sb[:], silu_r[:], ALU.mult).then_inc(silu_ready, 1)

            def take_ada0():
                dve.wait_ge(ada0_in, ADA0_IN)
                dve.wait_ge(setup_mm, 1)
                done(nc.vector.tensor_tensor(adaT[:, 0:ADA0, :], ps[:, 0, 0:ADA0 * B].rearrange("p (a b) -> p a b", b=B),
                                             b_ada_sb[:].unsqueeze(2).to_broadcast([P, ADA0, B]), ALU.add))
                done(nc.vector.tensor_scalar(adaT[:, 0:2, :], adaT[:, 0:2, :], 1.0, None, ALU.add))

            def take_w0():
                dve.wait_ge(setup_mm, 2)
                nc.vector.tensor_copy(w0_sb[:, :, C:W0], ps[:, 1, 0:NC * 2 * KVW].rearrange("p (k n) -> p k n", k=NC))\
                    .then_inc(w0_ready, 1)

            def constants():
                dve.wait_ge(ident_in, 16)
                dve.wait_ge(hide_in, HIDE_IN)
                nc.vector.tensor_copy(ident_b[:], ident[:]).then_inc(consts_ready, 1)
                nc.vector.tensor_copy(hide_q[:], hide_f[:, 0, :]).then_inc(consts_ready, 1)
                nc.vector.tensor_copy(hide_k[:], hide_f[:, 1, :]).then_inc(consts_ready, 1)
                nc.vector.tensor_copy(sel[:], sel_f[:]).then_inc(consts_ready, 1)

            def take_ada1_rows():
                dve.wait_ge(ada1_in, ADA1_IN)
                dve.wait_ge(setup_mm, 3)
                for n in range(3):
                    cols = slice(n * 2 * C, (n + 1) * 2 * C)
                    nc.vector.tensor_tensor(ada1_rows[:, cols], ps[0:B, TB + n, :], b_ada1_sb[:, cols],
                                            ALU.add).then_inc(rows_ready, 1)
                dve.wait_ge(rows_ready, 3)
                nc.vector.tensor_scalar(ada1_rows[:, 2 * C:4 * C], ada1_rows[:, 2 * C:4 * C], 1.0, None,
                                        ALU.add).then_inc(rows_ready, 1)

            def take_ada1():
                dve.wait_ge(setup_mm, 4)
                nc.vector.tensor_copy(adaT[:, ADA0:NADA, :], ps[:, OB, 0:ADA1 * B].rearrange("p (a b) -> p a b", b=B))\
                    .then_inc(ada1_ready, 1)
                dve.wait_ge(ada1_ready, 1)

            def mask_parts():
                nc.vector.tensor_copy(ident_r[:], ident[:])
                dve.wait_ge(mask_in, MASK_IN)
                done(nc.vector.tensor_scalar(bias_f[:], bias_f[:], LOWEST, None, ALU.max))
                done(nc.vector.tensor_copy(bias_hi[:], bias_f[:]))
                nc.vector.tensor_tensor(bias_lo[:], bias_f[:], bias_hi[:].bitcast(f32), ALU.subtract).then_inc(mask_ready, 1)

            def mask_count():
                done(nc.vector.tensor_scalar(biased_f, bias_f[:], 0.0, None, ALU.not_equal))
                nc.vector.tensor_reduce(biased_rows[:], biased_f.rearrange("p a t k -> p (a t k)"), AX.X,
                                        ALU.add).then_inc(rows_counted, 1)

            def take_flag():
                dve.wait_ge(count_done, 1)
                nc.vector.tensor_scalar(biased_flag[:], ps[0:1, TB, 0:1], 1.0, None, ALU.min).then_inc(flag_ready, 1)

            def norm_stats(u, L):
                step, finish = chain(stats_seq[L], u, SEQ_S)
                if L > 0:
                    dve.wait_ge(x_ready[L - 1], u * NT + NT)
                nc.vector.memset(wait_here[:], 0.0)
                for t in range(NT):
                    last = nc.vector.bn_stats(stats[:, t, :], xs[:, u, t, :])
                step(last)
                nc.vector.memset(wait_here[:], 0.0)
                for t in range(NT):
                    last = nc.vector.bn_aggr(mv[:, t, :], stats[:, t, :])
                step(last)
                nc.vector.tensor_copy(mean[:, u], mv[:, :, 0])
                nc.vector.tensor_scalar(var_eps[:, u], mv[:, :, 1], LN0_EPS if L == 0 else LN1_EPS, None,
                                        ALU.add).then_inc(var_ready[L], 1)
                finish()

            def norm_apply(u, L, step):
                if L == 2 and not (isinstance(u, int) and u == 0):
                    dve.wait_ge(hT_ready[2], u * NC)
                step(nc.vector.tensor_copy(ada_now[:], adaT[:, :, u]))
                dve.wait_ge(rstd_ready[L], u + 1)
                for t in range(NT):
                    nc.vector.tensor_scalar(xn[:, t, :], xs[:, u, t, :], mean[:, u, t:t + 1], rstd[:, u, t:t + 1],
                                            ALU.subtract, ALU.mult).then_inc(xn_ready[L], 1)

            def put_stack(step, source, dst, hi2, lo_at=None):
                hi = dst(0)
                step(nc.vector.tensor_copy(hi.bitcast(f32r), source))
                last = nc.vector.tensor_copy(dst(hi2), hi)
                if lo_at is not None:
                    last = nc.vector.tensor_tensor(dst(lo_at), source, hi, ALU.subtract)
                return last

            def slots(t, first, count):
                return lambda at: stack[:, t, first:first + count, at * D:(at + 1) * D]

            def rope_stack(u, t, step):
                nh = H + HKV
                dve.wait_ge(raw_ready[0], u * QKV_USES[0] + t + 1)
                xv = qk[:, t, 0:QK0].rearrange("p (h d) -> p h d", d=D)
                av = qk_a[:, t, 0:QK0].rearrange("p (h d) -> p h d", d=D)
                bv = qk_b[:, t, 0:QK0].rearrange("p (h d) -> p h d", d=D)
                cos = rope[:, t, 0, :].unsqueeze(1).to_broadcast([P, nh, D])
                nc.vector.tensor_tensor(av, xv, cos, ALU.mult)
                for lo, hi in ((0, D // 2), (D // 2, 0)):
                    sin = rope[:, t, 1, lo:lo + D // 2].unsqueeze(1).to_broadcast([P, nh, D // 2])
                    last = nc.vector.tensor_tensor(bv[:, :, lo:lo + D // 2], xv[:, :, hi:hi + D // 2], sin, ALU.mult)
                step(last)
                step(nc.vector.tensor_tensor(av, av, bv, ALU.add))
                for a in range(2):
                    src_q = qk_a[:, t, 0:C].rearrange("p (g a r d) -> p g a r d", a=2, r=4, d=D)[:, :, a]
                    dst_q = stack[:, t, 0:H, :].rearrange("p (g r a) s -> p g r a s", a=2, r=4)[:, :, :, a, :]
                    put_stack(step, src_q, lambda at: dst_q[:, :, :, at * D:(at + 1) * D], 2, 1)
                src_k = qk_a[:, t, C:QK0].rearrange("p (b a d) -> p b a d", a=2, d=D)
                dst_k = stack[:, t, H:2 * H, :].rearrange("p (b r) s -> p b r s", r=H // 2)[:, :, 0:2, :]
                put_stack(step, src_k, lambda at: dst_k[:, :, :, at * D:(at + 1) * D], 1, 2).then_inc(stack_ready[0], 1)

            def head_squares(u, t, step):
                dve.wait_ge(squares_ready, u * NT + t + 1)
                step(nc.vector.tensor_reduce(ss[:, t, :], qk_a[:, t, :].rearrange("p (h d) -> p h d", d=D),
                                             AX.X, ALU.add))

            def head_norms(step):
                i32 = mybir.dt.int32
                step(nc.vector.tensor_scalar(ss[:], ss[:], 1e-24, None, ALU.max))
                step(nc.vector.tensor_scalar(rs[:].bitcast(i32), ss[:].bitcast(i32), -0.5, float(0x5f3759df),
                                             ALU.mult, ALU.add))
                for _ in range(3):
                    step(nc.vector.scalar_tensor_tensor(nt_a[:], rs[:], -0.5, rs[:], ALU.mult, ALU.mult))
                    step(nc.vector.tensor_tensor(nt_b[:], nt_a[:], ss[:], ALU.mult))
                    step(nc.vector.scalar_tensor_tensor(rs[:], nt_b[:], 1.5, rs[:], ALU.add, ALU.mult))
                step(nc.vector.tensor_tensor(rs[:, :, 0:H], rs[:, :, 0:H],
                                             sm[:].unsqueeze(1).to_broadcast([P, NT, H]), ALU.mult))

            def norm_stack(t, step):
                step(nc.vector.tensor_tensor(
                    qk_b[:, t, :].rearrange("p (h d) -> p h d", d=D), qk[:, t, :].rearrange("p (h d) -> p h d", d=D),
                    rs[:, t, :].unsqueeze(2).to_broadcast([P, 2 * H, D]), ALU.mult))
                src_q = qk_b[:, t, 0:C].rearrange("p (h d) -> p h d", d=D)
                src_k = qk_b[:, t, C:2 * C].rearrange("p (h d) -> p h d", d=D)
                put_stack(step, src_q, slots(t, 0, H), 2).then_inc(stack_ready[1], 1)
                put_stack(step, src_k, slots(t, H, H), 1).then_inc(stack_ready[1], 1)

            def maxima(i, L, g, uses):
                for n in uses:
                    s = S_USES[L] * g + n
                    dve.wait_ge(s_done[L], i * S_ALL[L] + s + 1)
                    heads, t, nh = score_use(L, g, n)
                    nc.vector.tensor_reduce(negmax[:, heads:heads + nh, t],
                                            ps[:, SB + s % 2, :].rearrange("p (h k) -> p h k", h=nh),
                                            AX.X, ALU.max, negate=True).then_inc(max_done[L], 1)

            def cut_maxima(i, L, g):
                dve.wait_ge(max_done[L], i * S_ALL[L] + S_USES[L] * (g + 1))
                nm = negmax[:, GROUP * g:GROUP * (g + 1), :].rearrange("p h t -> p t h")
                nc.vector.tensor_copy(m_parts[:, g, :, :, 0].bitcast(f32r), nm).then_inc(max_cut[L], 1)
                dve.wait_ge(max_cut[L], i * NG + g + 1)
                nc.vector.tensor_tensor(m_parts[:, g, :, :, 1], nm, m_parts[:, g, :, :, 0],
                                        ALU.subtract).then_inc(m_ready[L], 1)

            def divide(i, L, g):
                dve.wait_ge(otr_done[L], i * NG + g + 1)
                ov = ps[:, MB, 0:2 * P].rearrange("p (t h s) -> p t h s", t=NT, h=GROUP)
                nc.vector.reciprocal(den[:], ov[:, :, :, D]).then_inc(den_ready[L], 1)
                dve.wait_ge(den_ready[L], i * NG + g + 1)
                for t in range(NT):
                    og = o[:, t, g * GROUP * D:(g + 1) * GROUP * D]
                    ogv, ovv = og.rearrange("p (h d) -> p h d", d=D), ov[:, t, :, 0:D]
                    dv = den[:, t, :].unsqueeze(2).to_broadcast([P, GROUP, D])
                    if L == 1:
                        ogv = og.rearrange("p (b a d) -> p a b d", a=2, d=D)
                        ovv = ovv.rearrange("p (a b) d -> p a b d", a=2)
                        dv = den[:, t, :].rearrange("p (a b) -> p a b", a=2).unsqueeze(3).to_broadcast([P, 2, 2, D])
                    last = nc.vector.tensor_tensor(ogv, ovv, dv, ALU.mult)
                last.then_inc(o_ready[L], 1)

            def residual(i, L, bank):
                if L == 1:
                    dve.wait_ge(xb_ready[1], i + 1)
                dve.wait_ge(proj_done[L], i + 1)
                new = ps[:, bank, :].rearrange("p (t c) -> p t c", t=NT)
                if L == 1:
                    nc.vector.tensor_tensor(scaled[:], new, gamma[:, i, 0, :].unsqueeze(1).to_broadcast([P, NT, C]),
                                            ALU.mult).then_inc(scaled_ready[1], 1)
                    dve.wait_ge(scaled_ready[1], i + 1)
                    new = scaled[:]
                for t in range(NT):
                    nc.vector.tensor_tensor(xs[:, i, t, :], xs[:, i, t, :], new[:, t, :],
                                            ALU.add).then_inc(x_ready[L], 1)

            def prepare(u, L):
                norm_stats(u, L)
                take_ada0()
                take_w0()
                step, finish = chain(pre_seq[L], u, SEQ_P[L])
                norm_apply(u, L, step)
                dve.wait_ge(rope_in, 16)
                dve.wait_ge(pads_set, 4)
                for t in range(NT):
                    rope_stack(u, t, step)
                finish()
                dve.wait_ge(scale_in, 16)
                nc.vector.tensor_scalar(sm_l[:], scale_sb[:], 4.605170185988092, None, ALU.min).then_inc(sm_min, 1)
                constants()
                take_ada1_rows()

            def attention(i, L, before, u, LN):
                pre, pre_finish = chain(pre_seq[LN], u, SEQ_P[LN])
                uses = S_USES[L]
                maxima(i, L, 1, range(0, 2))
                norm_apply(u, LN, pre)
                if before is not None:
                    divide(before[1], before[0], NG - 1)
                maxima(i, L, 1, range(2, uses))
                cut_maxima(i, L, 1)
                if before is None:
                    norm_stats(2, 0)
                    mask_parts()
                    mask_count()
                maxima(i, L, 2, range(uses))
                cut_maxima(i, L, 2)
                if before is None:
                    norm_stats(3, 0)
                    take_ada1()
                if LN == 0:
                    dve.wait_ge(fill_done[L], (i + 1) * FILLS[L])
                    rope_stack(u, 0, pre)
                if LN == 1:
                    head_squares(u, 0, pre)
                if LN == 1:
                    head_squares(u, 1, pre)
                maxima(i, L, 3, range(uses))
                cut_maxima(i, L, 3)
                divide(i, L, 0)
                if LN == 0:
                    rope_stack(u, 1, pre)
                if LN == 1:
                    head_norms(pre)
                    dve.wait_ge(fill_done[L], (i + 1) * FILLS[L])
                    norm_stack(0, pre)
                    norm_stack(1, pre)
                pre_finish()
                divide(i, L, 1)
                if before is not None:
                    residual(before[1], before[0], PB)
                if LN < 2:
                    maxima(u, LN, 0, range(S_USES[LN]))
                    cut_maxima(u, LN, 0)
                if LN == 2:
                    dve.wait_ge(st_done[1], B * H)
                    split_h(u)
                divide(i, L, 2)
                if before is None:
                    take_flag()
                if before is not None:
                    norm_stats(before[1], before[0] + 1)

            def split_h(i):
                dve.wait_ge(hT_ready[2], (i + 1) * NC)
                nc.vector.tensor_copy(h_hi, hT[:]).then_inc(h_hi_ready, 1)
                dve.wait_ge(h_hi_ready, i + 1)
                nc.vector.tensor_tensor(h_lo, hT[:], h_hi.bitcast(f32), ALU.subtract).then_inc(h_parts, 1)

            def split_g(i, hidden):
                for f in hidden:
                    dve.wait_ge(gelu_done, i * NF + f + 1)
                    nc.vector.tensor_copy(g_hi[:, f, :], gT[:, f, :]).then_inc(g_hi_ready, 1)
                    dve.wait_ge(g_hi_ready, i * NF + f + 1)
                    nc.vector.tensor_tensor(g_lo[:, f, :], gT[:, f, :], g_hi[:, f, :].bitcast(f32),
                                            ALU.subtract).then_inc(g_parts, 1)

            def norm_mlp(i):
                pre, pre_finish = chain(pre_seq[2], i, SEQ_P[2])
                norm_apply(i, 2, pre)
                pre_finish()

            def output(i):
                dve.wait_ge(xb_ready[2], i + 1)
                for t in range(NT):
                    dve.wait_ge(fc2_done, i * NT + t + 1)
                    nc.vector.tensor_tensor(scaled[:, t, :], ps[:, SB + t, 0:C], gamma[:, i, 1, :], ALU.mult)\
                        .then_inc(scaled_ready[2], 1)
                    dve.wait_ge(scaled_ready[2], i * NT + t + 1)
                    nc.vector.tensor_tensor(xs[:, i, t, :], scaled[:, t, :], xs[:, i, t, :],
                                            ALU.add).then_inc(y_ready, 1)

            dve.wait_ge(x_first, 16)
            prepare(0, 0)
            maxima(0, 0, 0, range(S_USES[0]))
            cut_maxima(0, 0, 0)
            dve.wait_ge(x_rest, 16)
            norm_stats(1, 0)
            attention(0, 0, None, 1, 0)
            with dve.Fori(1, B - 1) as i:
                attention(i, 0, (0, i - 1), i + 1, 0)
            dve.wait_ge(gamma_in, 16)
            dve.wait_ge(sm_ready, 1)
            attention(B - 1, 0, (0, B - 2), 0, 1)
            attention(0, 1, (0, B - 1), 1, 1)
            with dve.Fori(1, B - 1) as i:
                attention(i, 1, (1, i - 1), i + 1, 1)
            attention(B - 1, 1, (1, B - 2), 0, 2)
            norm_mlp(1)
            divide(B - 1, 1, NG - 1)
            split_g(0, range(0, 4))
            residual(B - 1, 1, OB)
            norm_stats(B - 1, 2)
            split_g(0, range(4, NF))
            split_h(1)
            output(0)
            with dve.Fori(1, B - 1) as i:
                norm_mlp(i + 1)
                split_g(i, range(NF))
                split_h(i + 1)
                output(i)
            split_g(B - 1, range(NF))
            output(B - 1)

        @block.tensor
        def _(pe):
            mm, tr = nc.tensor.matmul, nc.tensor.transpose

            def setup_layer0():
                pe.wait_ge(cond_in, 16)
                pe.wait_ge(ada0_in, ADA0_IN)
                for a in range(ADA0):
                    for k in range(NC):
                        last = mm(ps[:, 0, a * B:(a + 1) * B], w_ada_sb[:, k, a * P:(a + 1) * P], condT_sb[:, k, :],
                                  start=k == 0, stop=k == NC - 1)
                last.then_inc(setup_mm, 1)
                pe.wait_ge(w0_in, W0_IN)
                for k in range(NC):
                    last = mm(ps[:, 1, k * 2 * KVW:(k + 1) * 2 * KVW], wkd_sb[:, k * P:(k + 1) * P], wkuv_sb[:],
                              start=True, stop=True)
                last.then_inc(setup_mm, 1)
                pe.wait_ge(ident_in, 16)

            def setup_layer1():
                pe.wait_ge(silu_ready, 1)
                pe.wait_ge(ada1_in, ADA1_IN)
                for n in range(3):
                    for k in range(NC):
                        last = mm(ps[0:B, TB + n, :], siluT[:, k, :], w_ada1_sb[:, k, n * 2 * C:(n + 1) * 2 * C],
                                  start=k == 0, stop=k == NC - 1)
                last.then_inc(setup_mm, 1)

            def transposed_ada1():
                pe.wait_ge(fill_ready[0], FILLS[0])
                for a in range(ADA1):
                    last = tr(ps[:, OB, a * B:(a + 1) * B], ada1_rows[:, 2 * C + a * P:2 * C + (a + 1) * P],
                              ident[0:B, 0:B])
                last.then_inc(setup_mm, 1)

            def transposed_norm(u, L, before=None):
                if before is not None:
                    pe.wait_ge(fill_ready[before[0]], before[1] * FILLS[before[0]] + FILLS_AHEAD)
                for t in range(NT):
                    pe.wait_ge(xn_ready[L], u * NT + t + 1)
                    for c in range(NC):
                        last = tr(ps[:, XB, c * T + t * P:c * T + (t + 1) * P], xn[:, t, c * P:(c + 1) * P], ident[:])
                last.then_inc(xnT_done[L], 1)

            def project_qkv(u, L, n, before=None):
                if n == 0:
                    pe.wait_ge(hT_ready[L], u * NC + NC)
                if n > 0:
                    pe.wait_ge(raw_ready[L], u * QKV_USES[L] + n)
                if n == 2:
                    pe.wait_ge(fill_ready[before[0]], (before[1] + 1) * FILLS[before[0]])
                w = w0_sb if L == 0 else wqkv_sb
                if L == 0:
                    parts = ((n, 0, 0, W0),)
                elif n < NT:
                    parts = ((n, 0, 0, 2 * C),)
                else:
                    parts = tuple((t, t * C, 2 * C, 3 * C) for t in range(NT))
                for t, col, n0, n1 in parts:
                    for c in range(NC):
                        last = mm(ps[:, XB, col:col + n1 - n0], hT[:, c, t * P:(t + 1) * P], w[:, c, n0:n1],
                                  start=c == 0, stop=c == NC - 1)
                last.then_inc(qkv_done[L], 1)

            def transposed_stacks(u, L, n, other=None, first=False):
                if n == 0:
                    if L == 0:
                        pe.wait_ge(stack_ready[0], u * NT + NT)
                    else:
                        pe.wait_ge(stack_ready[1], (u + 1) * 2 * NT)
                        pe.wait_ge(lo_ready, (u + 1) * 2 * NT)
                    pe.wait_ge(raw_ready[L], (u + 1) * QKV_USES[L])
                elif first:
                    if n == FILLS_AHEAD - 1:
                        pe.wait_ge(fill_ready[L], 1)
                elif n == 1:
                    pe.wait_ge(max_done[other[0]], (other[1] + 1) * S_ALL[other[0]])
                elif n == FILLS_AHEAD:
                    if L == 0 and isinstance(u, int) and u == 0:
                        pass
                    elif not isinstance(u, int) or u > 0:
                        pe.wait_ge(oT_evac[L], u * NG)
                    else:
                        pe.wait_ge(oT_evac[0], B * NG)
                elif n == FILLS_AHEAD + 1:
                    if other[0] < 2:
                        pe.wait_ge(raw_ready[other[0]], other[1] * QKV_USES[other[0]] + NT)
                    else:
                        pe.wait_ge(hT_ready[2], other[1] * NC + NC)
                elif n == FILLS_AHEAD + 2:
                    pe.wait_ge(fill_ready[L], u * FILLS[L] + FILLS_AHEAD + 1)
                else:
                    pe.wait_ge(fill_ready[L], u * FILLS[L] + n)
                bank = FILL_BANK_0[n] if first else FILL_BANK[n]
                for j, blk in enumerate(FILL_BLOCKS[L][n]):
                    for t in range(NT):
                        last = tr(ps[:, bank, j * T + t * P:j * T + (t + 1) * P],
                                  stack[:, t, 2 * blk:2 * blk + 2, :].rearrange("p h s -> p (h s)"), ident[:])
                last.then_inc(fill_done[L], 1)

            def place(L, h):
                h = head_at(L, h)
                if L == 0:
                    return (h // 8) * 4 + h % 4, H // 2 + 4 * (h // 8), SLOT * ((h // 4) % 2)
                return h // 2, H // 2 + h // 2, SLOT * (h % 2)

            def scores(i, L, g, n, masked):
                s = S_USES[L] * g + n
                if n == 0:
                    pe.wait_ge(fill_ready[L], i * FILLS[L] + fills_for(L, g))
                if s >= 2 or not isinstance(i, int) or i > 0:
                    pe.wait_ge(max_done[L], i * S_ALL[L] + s - 1)
                elif L == 1:
                    pe.wait_ge(max_done[0], B * S_ALL[0])
                bank = ps[:, SB + s % 2, :]
                heads, t, nh = score_use(L, g, n)
                keys = P if L == 0 and t == 0 else T
                if L == 0:
                    hide = hide_q[:, 0:P] if t == 0 else hide_q[:, P:3 * P]
                    mm(bank, ident_b[:], hide.unsqueeze(1).to_broadcast([P, nh, keys]), start=True, stop=False)
                elif masked:
                    for j, part in enumerate((bias_hi, bias_lo)):
                        mm(bank, ident_r[:], part[:, 0, t, :].unsqueeze(1).to_broadcast([P, nh, keys]),
                           start=j == 0, stop=False)
                for j in range(nh):
                    qb, kb, half = place(L, heads + j)
                    last = mm(bank[:, j * keys:(j + 1) * keys],
                              qkT[half:half + STACK, qb, t * P:(t + 1) * P],
                              qkT[half:half + STACK, kb, 0:keys], start=not masked,
                              stop=not masked or j == nh - 1)
                last.then_inc(s_done[L], 1)

            def transposed_maxima(i, L, g, before):
                pe.wait_ge(m_ready[L], i * NG + g + 1)
                if g == 0 and before is not None:
                    pe.wait_ge(o_ready[before[0]], before[1] * NG + NG - 1)
                if g == 1 and before is not None:
                    pe.wait_ge(oc_ready[before[0]], before[1] + 1)
                if g == 3:
                    pe.wait_ge(o_ready[L], i * NG + 1)
                for at, t in enumerate((0, 1, 1) if L == 0 else (0, 1)):
                    last = tr(ps[0:2 * GROUP, MB, at * P:(at + 1) * P],
                              m_parts[:, g, t].rearrange("p h a -> p (h a)"), ident[:])
                last.then_inc(mT_done[L], 1)

            def scores_T(i, L, g, j, masked):
                n = GROUP * g + j
                if j == 0:
                    pe.wait_ge(mT_ready[L], i * NG + g + 1)
                if n >= NTB:
                    pe.wait_ge(exp_done[L], i * H + n - NTB + 1)
                qb, kb, half = place(L, n)
                bank = ps[:, TB + n % NTB, :]
                if L == 0:
                    mm(bank[:, 0:3 * P], ident_b[:], hide_k[:], start=True, stop=False)
                    mm(bank[:, 0:3 * P], sel[:, j, :], mT[:, g % 2, :], start=False, stop=False)
                    spans = ((0, 0, 0, T), (1, T, P, T))
                else:
                    if masked:
                        for a, part in enumerate((bias_hi, bias_lo)):
                            mm(bank, ident_r[:], part[:, 1].rearrange("p t q -> p (t q)"), start=a == 0, stop=False)
                    mm(bank, sel[:, j, :], mT[:, g % 2, 0:T].unsqueeze(1).to_broadcast([2 * GROUP, 2, T]),
                       start=not masked, stop=False)
                    spans = ((0, 0, 0, T), (1, T, 0, T))
                for kt, col, q0, q1 in spans:
                    last = mm(bank[:, col:col + q1 - q0], qkT[half:half + STACK, kb, kt * P:(kt + 1) * P],
                              qkT[half:half + STACK, qb, q0:q1], start=False, stop=kt == 1)
                last.then_inc(st_done[L], 1)

            def outputs(i, L, g, before):
                if g == 0:
                    pe.wait_ge(v_ready[L], i + 1)
                if g == 0:
                    pe.wait_ge(fill_ready[L], (i + 1) * FILLS[L])
                if g > 0:
                    pe.wait_ge(oT_evac[L], i * NG + g)
                pe.wait_ge(exp_done[L], i * H + GROUP * (g + 1))
                for kt in range(2):
                    q0 = P if L == 0 and kt == 1 else 0
                    for j in range(GROUP):
                        vh = g if L == 0 else head_at(L, GROUP * g + j)
                        last = mm(ps[2 * D * j:2 * D * (j + 1), OB, q0:T], vaug[L][:, kt, vh, :],
                                  prob[:, g % 2, j, kt * T:kt * T + T - q0], start=kt == 0, stop=kt == 1)
                last.then_inc(av_done[L], 1)

            def transposed_outputs(i, L, g, after=None):
                pe.wait_ge(oT_evac[L], i * NG + g + 1)
                if g < 2:
                    pe.wait_ge(mT_ready[L], i * NG + g + 3)
                elif after is not None:
                    pe.wait_ge(mT_ready[after[0]], after[1] * NG + 1)
                else:
                    pe.wait_ge(o_ready[L], i * NG + g)
                for t in range(NT):
                    last = tr(ps[:, MB, t * P:(t + 1) * P], oT_raw[:, g % 2, t * P:(t + 1) * P], ident[:])
                last.then_inc(otr_done[L], 1)

            def prepare(u, L):
                transposed_norm(u, L)
                pe.wait_ge(w0_ready, 1)
                for n in range(QKV_USES[L]):
                    project_qkv(u, L, n)
                setup_layer1()
                for n in range(FILLS_AHEAD):
                    transposed_stacks(u, L, n, first=True)
                pe.wait_ge(consts_ready, 4)
                pe.wait_ge(rows_ready, 4)

            def gathered_outputs(i, L):
                pe.wait_ge(o_ready[L], i * NG + NG)
                for c in range(NC):
                    for t in range(NT):
                        last = tr(ps[:, MB, c * T + t * P:c * T + (t + 1) * P], o[:, t, c * P:(c + 1) * P], ident[:])
                last.then_inc(oc_done[L], 1)

            def project_outputs(i, L, after=None):
                pe.wait_ge(oc_ready[L], i + 1)
                if after is None:
                    bank = OB
                    pe.wait_ge(oT_evac[L], i * NG + NG)
                else:
                    bank = PB
                    pe.wait_ge(exp_done[after[0]], after[1] * H + LAST_IN_PB + 1)
                w = wo_sb if L == 0 else wproj_sb
                for t in range(NT):
                    for c in range(NC):
                        last = mm(ps[:, bank, t * C:(t + 1) * C], oT[:, c, t * P:(t + 1) * P], w[:, c, :],
                                  start=c == 0, stop=c == NC - 1)
                last.then_inc(proj_done[L], 1)

            def attention(i, L, before, u, LN, masked=True, masked_next=True):
                uses = S_USES[L]
                for g in range(NG):
                    transposed_maxima(i, L, g, before)
                    if g + 1 < NG:
                        scores(i, L, g + 1, 0, masked)
                        scores(i, L, g + 1, 1, masked)
                    if g == 1 and LN < 2:
                        project_qkv(u, LN, 1, (L, i))
                    if g == 3 and LN == 1:
                        project_qkv(u, LN, 2, (L, i))
                    for j in range(GROUP):
                        if g >= 2 and j == 1:
                            transposed_outputs(i, L, g - 2)
                        scores_T(i, L, g, j, masked)
                        if g + 1 < NG and j < uses - 2:
                            scores(i, L, g + 1, 2 + j, masked)
                        if (g, j) == (0, 0):
                            transposed_stacks(i, L, 5, (LN, u))
                        if (g, j) == (0, 1):
                            transposed_norm(u, LN, (L, i))
                        if (g, j) == (0, 0) and before is not None:
                            transposed_outputs(before[1], before[0], NG - 1, (L, i))
                        if L == 1 and (g, j) in ((1, 1), (1, 2)):
                            transposed_stacks(i, L, 5 + j, (LN, u))
                        if LN == 0 and g == 3 and j >= 1:
                            transposed_stacks(u, LN, j - 1, (L, i))
                    if g == 0 and before is not None:
                        gathered_outputs(before[1], before[0])
                    if g == 0 and LN < 2:
                        project_qkv(u, LN, 0, (L, i))
                    if g == 1 and before is None:
                        transposed_ada1()
                        pe.wait_ge(ada1_ready, 1)
                    if g in (1, 2):
                        outputs(i, L, g - 1, before)
                if before is not None:
                    project_outputs(before[1], before[0], (L, i))
                if LN < 2:
                    for n in range(3 * (1 - LN), FIRST_FILLS[LN]):
                        transposed_stacks(u, LN, n, (L, i))
                outputs(i, L, NG - 2, before)
                if LN < 2:
                    for n in range(S_USES[LN]):
                        scores(u, LN, 0, n, masked_next)
                        if n == 1:
                            transposed_stacks(u, LN, FIRST_FILLS[LN])
                    transposed_stacks(u, LN, FIRST_FILLS[LN] + 1)
                transposed_outputs(i, L, NG - 2)
                if before is not None:
                    pe.wait_ge(x_ready[before[0]], (before[1] + 1) * NT)
                outputs(i, L, NG - 1, before)
                if LN < 2:
                    for n in range(FIRST_FILLS[LN] + 2, FILLS_AHEAD):
                        transposed_stacks(u, LN, n)

            def fc1(i, hidden):
                for f in hidden:
                    if f == 0:
                        pe.wait_ge(h_parts, i + 1)
                    if f >= len(GB):
                        pe.wait_ge(gelu_done, i * NF + f - len(GB) + 1)
                    for c in range(NC):
                        for w, h in ((w1_lo, h_hi), (w1_hi, h_hi), (w1_hi, h_lo)):
                            last = mm(ps[:, GB[f % len(GB)], 0:T], w[:, c, f * P:(f + 1) * P], h[:, c, :],
                                      start=c == 0 and w is w1_lo, stop=c == NC - 1 and h is h_lo)
                    last.then_inc(fc1_done, 1)

            def fc2(i):
                if not isinstance(i, int) or i > 0:
                    pe.wait_ge(scaled_ready[2], i * NT)
                for t in range(NT):
                    for f in range(NF):
                        if t == 0:
                            pe.wait_ge(g_parts, i * NF + f + 1)
                        for g, w in ((g_lo, w2_hi), (g_hi, w2_hi), (g_hi, w2_lo)):
                            last = mm(ps[:, SB + t, 0:C], g[:, f, t * P:(t + 1) * P], w[:, f, :],
                                      start=f == 0 and g is g_lo, stop=f == NF - 1 and w is w2_lo)
                    last.then_inc(fc2_done, 1)

            setup_layer0()
            prepare(0, 0)
            for n in range(S_USES[0]):
                scores(0, 0, 0, n, True)
            pe.wait_ge(fill_ready[0], FILLS_AHEAD)
            attention(0, 0, None, 1, 0)
            pe.wait_ge(mask_ready, 1)
            pe.wait_ge(rows_counted, 1)
            mm(ps[0:1, TB, 0:1], biased_rows[:], ones[:], start=True, stop=True).then_inc(count_done, 1)
            pe.wait_ge(late_in, LATE_IN)
            pe.wait_ge(flag_ready, 1)
            with pe.Fori(1, B - 1) as i:
                attention(i, 0, (0, i - 1), i + 1, 0)
            biased = nc.tensor.value_load(biased_flag[0:1, 0:1], min_val=0, max_val=1)

            def layer1(masked):
                attention(B - 1, 0, (0, B - 2), 0, 1, True, masked)
                attention(0, 1, (0, B - 1), 1, 1, masked, masked)
                with pe.Fori(1, B - 1) as i:
                    attention(i, 1, (1, i - 1), i + 1, 1, masked, masked)
                attention(B - 1, 1, (1, B - 2), 0, 2, masked, masked)

            with pe.If(biased):
                layer1(True)
            with pe.Else():
                layer1(False)
            pe.wait_ge(w_lo_ready, 2)
            fc1(0, range(0, 2))
            transposed_outputs(B - 1, 1, NG - 1)
            fc1(0, range(2, 4))
            gathered_outputs(B - 1, 1)
            fc1(0, range(4, 6))
            project_outputs(B - 1, 1)
            fc1(0, range(6, NF))
            transposed_norm(1, 2)
            fc2(0)
            with pe.Fori(1, B - 1) as i:
                fc1(i, range(NF))
                transposed_norm(i + 1, 2)
                fc2(i)
            fc1(B - 1, range(NF))
            fc2(B - 1)


def score_use(L, g, n):
    if L == 0:
        return (GROUP * g, 0, GROUP) if n == 0 else (GROUP * g + 2 * (n - 1), 1, 2)
    return GROUP * g + 2 * (n // 2), n % 2, 2


def fills_for(L, g):
    return FILLS[0] // 2 * (1 + g // 2) if L == 0 else 2 * (g + 1)


def head_at(L, n):
    return n if L == 0 else n // GROUP * GROUP + (0, 2, 1, 3)[n % GROUP]


def kernel(x, cond_2048, mask_1x1xSxS_ff0, L0_cond_W_ada, L0_cond_b_ada, L0_cond_Wq, L0_cond_Wkd, L0_cond_Wku,
           L0_cond_Wvu, L0_cond_Wo, L1_cond_Wqkv, L1_cond_q_bias, L1_cond_v_bias, L1_cond_scale_mul_log,
           L1_cond_Wproj, L1_cond_bproj, L1_cond_Wada, L1_cond_bada, L1_cond_Wfc1, L1_cond_bfc1, L1_cond_Wfc2,
           L1_cond_bfc2):
    import numpy as np
    import concourse.bacc as bacc
    from concourse.bass_utils import run_bass_kernel_spmd

    def arr(a):
        return np.ascontiguousarray(np.asarray(a))

    pos = np.arange(T)
    freqs = (1.0 / np.float32(10000.0) ** (np.arange(0, D, 2, dtype=np.float32) / D)).astype(np.float32)
    angle = pos.astype(np.float32)[:, None] * freqs[None, :]
    rope = np.zeros((T, 2, D), np.float32)
    rope[:, 0, :] = np.concatenate([np.cos(angle), np.cos(angle)], -1)
    rope[:, 1, :] = np.concatenate([-np.sin(angle), np.sin(angle)], -1)
    blk = pos // 128
    hidden = ((np.abs(pos[None, :] - pos[:, None]) > 32) & ~(pos % 64 == 0)[None, :]) | (blk[None, :] > blk[:, None])
    hide = np.where(hidden, np.float32(NEG), np.float32(0.0)).astype(np.float32)
    hide_q = np.concatenate([hide[0:P, 0:P], hide[P:T, :]], 1)
    hide_k = np.concatenate([hide.T[0:P, :], hide.T[P:T, P:T]], 1)
    sel = np.zeros((2 * GROUP, GROUP, P), np.float32)
    for j in range(GROUP):
        sel[2 * j:2 * j + 2, j, :] = 1.0

    mask = arr(mask_1x1xSxS_ff0).reshape(T, T)
    arrays = {
        "x": arr(x),
        "condT": arr(arr(cond_2048).T),
        "w_adaT": arr(arr(L0_cond_W_ada).T),
        "w_ada1T": arr(arr(L1_cond_Wada).T),
        "b_adaT": arr(arr(L0_cond_b_ada).reshape(ADA0, P).T),
        "b_ada1": arr(L1_cond_bada),
        "wqT": arr(arr(L0_cond_Wq).T),
        "wkd": arr(L0_cond_Wkd),
        "wkuvT": arr(np.concatenate([arr(L0_cond_Wku), arr(L0_cond_Wvu)], 0).T),
        "woT": arr(arr(L0_cond_Wo).T),
        "wqkvT": arr(arr(L1_cond_Wqkv).T),
        "q_bias": arr(L1_cond_q_bias),
        "v_bias": arr(L1_cond_v_bias),
        "scale_log": arr(L1_cond_scale_mul_log).reshape(H),
        "wprojT": arr(arr(L1_cond_Wproj).T),
        "bproj": arr(L1_cond_bproj),
        "wfc1T": arr(arr(L1_cond_Wfc1).T),
        "bfc1T": arr(arr(L1_cond_bfc1).reshape(NF, P).T),
        "wfc2T": arr(arr(L1_cond_Wfc2).T),
        "bfc2": arr(L1_cond_bfc2),
        "bias_q": mask,
        "bias_k": arr(mask.T),
        "ident_d": np.eye(P, dtype=np.float32),
        "rope_d": rope,
        "hide_q_d": arr(hide_q),
        "hide_k_d": arr(hide_k),
        "sel_d": sel,
    }
    nc = bacc.Bacc("TRN2", target_bir_lowering=False, num_devices=1)
    aps = {n: nc.dram_tensor("in_" + n, a.shape, mybir.dt.from_np(a.dtype), kind="ExternalInput").ap()
           for n, a in arrays.items()}
    out = nc.dram_tensor("out_0", (B, T, C), mybir.dt.float32, kind="ExternalOutput").ap()
    build(nc, out=out, **aps)
    r = run_bass_kernel_spmd(nc, [{"in_" + n: a for n, a in arrays.items()}], core_ids=[0])
    return r.results[0]["out_0"]
```
